# Optimizing a Trainium2 kernel written in Bass

```python
import numpy as np
import jax
import jax.numpy as jnp

def _softmax(x, axis=-1):
    return jax.nn.softmax(x, axis=axis)

def _gelu(x):
    return jax.nn.gelu(x, approximate=True)

def _silu(x):
    return jax.nn.silu(x)

def _sigmoid(x):
    return jax.nn.sigmoid(x)

def _layernorm(x, axis=-1, eps=1e-05):
    m = jnp.mean(x, axis=axis, keepdims=True)
    v = jnp.var(x, axis=axis, keepdims=True)
    return (x - m) / jnp.sqrt(v + eps)

def _scatter_add(tgt, idx, src, axis=0):
    return tgt.at[idx].add(src)

def _segment_sum(src, seg, n):
    return jax.ops.segment_sum(src, seg, n)
kernel_name = 'mk_xattn_ffn_d1_seqx_r2_de086d'

def setup_inputs(seed: int=0):
    np.random.seed(seed)
    _w = jnp.asarray

    def _rec_inputs():
        import jax
        import jax.numpy as jnp
        _rk = jax.random.key(seed)
        x = 6.313e-05 + 0.9998 * jax.random.normal(jax.random.fold_in(_rk, 1), (8, 512, 512), jnp.float32)
        _lenS = 512 - jax.random.randint(jax.random.fold_in(_rk, 7), (8,), 0, max(1, 512 // 4) + 1, jnp.int32)
        _lenS2 = 77 - jax.random.randint(jax.random.fold_in(_rk, 8), (8,), 0, max(1, 77 // 4) + 1, jnp.int32)
        _ctx_1024P = jax.random.normal(jax.random.fold_in(_rk, 11), (8, 16, 512), jnp.float32)
        _ctx_1024c = jax.random.dirichlet(jax.random.fold_in(_rk, 511), 0.3 * jnp.ones((16,), jnp.float32), (8, 77))
        _ctx_1024t = jnp.einsum('bsk,bkd->bsd', _ctx_1024c, _ctx_1024P)
        _ctx_1024t = _ctx_1024t * jax.lax.rsqrt(jnp.mean(jnp.square(_ctx_1024t)) + 1e-12) * 0.953939
        ctx_1024 = -0.000214406 + 1.00034 * (_ctx_1024t + 0.3 * jax.random.normal(jax.random.fold_in(_rk, 611), (8, 77, 512), jnp.float32))
        return (x, ctx_1024)
    x, ctx_1024 = _rec_inputs()

    def _L0_xattn_setup():
        import jax, jax.numpy as jnp
        import numpy as np
        from jax import lax
        BIG = jnp.float32(1e+30)

        def _pairwise_euclidean(a, b):
            aa = jnp.sum(a * a, axis=-1)[:, None]
            bb = jnp.sum(b * b, axis=-1)[None, :]
            ab = a @ b.T
            return jnp.sqrt(jnp.maximum(aa + bb - 2.0 * ab, 0.0))

        def _dtw_cost(D):
            row0 = jnp.cumsum(D[0])

            def row_step(prev_row, d_row):
                first = d_row[0] + prev_row[0]

                def col_step(left, inp):
                    d_ij, up, diag = inp
                    r = d_ij + jnp.minimum(jnp.minimum(up, left), diag)
                    return (r, r)
                _, rest = lax.scan(col_step, first, (d_row[1:], prev_row[1:], prev_row[:-1]))
                row = jnp.concatenate([first[None], rest])
                return (row, row)
            _, rows = lax.scan(row_step, row0, D[1:])
            return jnp.concatenate([row0[None], rows], axis=0)

        def _backtrack(R, T1, T2):
            L = T1 + T2 - 1

            def step(carry, _):
                i, j, done = carry
                valid = jnp.logical_not(done)
                cd = jnp.where((i > 0) & (j > 0), R[jnp.maximum(i - 1, 0), jnp.maximum(j - 1, 0)], BIG)
                cu = jnp.where(i > 0, R[jnp.maximum(i - 1, 0), j], BIG)
                cl = jnp.where(j > 0, R[i, jnp.maximum(j - 1, 0)], BIG)
                choice = jnp.argmin(jnp.stack([cd, cu, cl]))
                ni = jnp.where(choice <= 1, i - 1, i)
                nj = jnp.where((choice == 0) | (choice == 2), j - 1, j)
                at_origin = (i == 0) & (j == 0)
                ni = jnp.where(at_origin, 0, ni)
                nj = jnp.where(at_origin, 0, nj)
                return ((ni, nj, done | at_origin), (i, j, valid))
            init = (jnp.int32(T1 - 1), jnp.int32(T2 - 1), jnp.bool_(False))
            _, (i_idx, j_idx, valid) = lax.scan(step, init, None, length=L)
            return (i_idx, j_idx, valid)

        def _align_one(small, large):
            T_small, d = small.shape
            T_large = large.shape[0]
            D = _pairwise_euclidean(small, large)
            R = _dtw_cost(D)
            i_idx, j_idx, valid = _backtrack(R, T_small, T_large)
            contrib = small[i_idx] * valid[:, None].astype(small.dtype)
            expanded = jnp.zeros((T_large, d), dtype=small.dtype).at[j_idx].add(contrib)
            return expanded
        key = jax.random.key(seed)
        k1, k2 = jax.random.split(key)
        teacher = jax.random.normal(k1, (16, 200, 512), dtype=jnp.float32)
        student = jax.random.normal(k2, (16, 300, 512), dtype=jnp.float32)
        return {'teacher_features': teacher, 'student_features': student}
    _L0_xattn_all = _L0_xattn_setup()
    _L0_xattn_in = {k: v for k, v in _L0_xattn_all.items() if k in ()}
    del _L0_xattn_all

    def _L0_ffn_setup():
        import jax, jax.numpy as jnp
        import numpy as np
        EPS = 1e-08

        def _ste(x, q):
            return x + jax.lax.stop_gradient(q - x)

        def quant_act_uint8(x):
            s = jax.lax.stop_gradient(jnp.maximum(jnp.max(x), EPS)) / 255.0
            q = jnp.clip(jnp.round(x / s), 0.0, 255.0) * s
            return (_ste(x, q), s)

        def quant_weight_int8_perchannel(w):
            s = jax.lax.stop_gradient(jnp.maximum(jnp.max(jnp.abs(w), axis=1, keepdims=True), EPS)) / 127.0
            q = jnp.clip(jnp.round(w / s), -128.0, 127.0) * s
            return (_ste(w, q), s[:, 0])

        def quant_bias_int32(b, s_in, s_w):
            s = jax.lax.stop_gradient(s_in * s_w)
            q = jnp.round(b / s) * s
            return _ste(b, q)

        def quant_linear(x, w, b):
            xq, s_in = quant_act_uint8(x)
            wq, s_w = quant_weight_int8_perchannel(w)
            bq = quant_bias_int32(b, s_in, s_w)
            return jnp.einsum('btd,fd->btf', xq, wq) + bq
        key = jax.random.key(seed)
        k1, k2, k3, k4, k5 = jax.random.split(key, 5)
        B, S, D, F = (4, 1024, 512, 2048)
        return {'x': jax.random.normal(k1, (B, S, D), dtype=jnp.float32), 'w1': jax.random.normal(k2, (F, D), dtype=jnp.float32) * (1.0 / np.sqrt(D)), 'b1': jax.random.normal(k3, (F,), dtype=jnp.float32) * 0.01, 'w2': jax.random.normal(k4, (D, F), dtype=jnp.float32) * (1.0 / np.sqrt(F)), 'b2': jax.random.normal(k5, (D,), dtype=jnp.float32) * 0.01}
    _L0_ffn_all = _L0_ffn_setup()
    _L0_ffn_in = {k: v for k, v in _L0_ffn_all.items() if k in ('w1', 'b1', 'w2', 'b2')}
    del _L0_ffn_all
    return {'x': x, 'ctx_1024': ctx_1024, 'L0_ffn_w1': _L0_ffn_in['w1'], 'L0_ffn_b1': _L0_ffn_in['b1'], 'L0_ffn_w2': _L0_ffn_in['w2'], 'L0_ffn_b2': _L0_ffn_in['b2']}

def reference(x, ctx_1024, L0_ffn_w1, L0_ffn_b1, L0_ffn_w2, L0_ffn_b2):
    import jax
    import jax.numpy as jnp

    def _L0_xattn_ref(teacher_features, student_features):
        import jax, jax.numpy as jnp
        import numpy as np
        from jax import lax
        BIG = jnp.float32(1e+30)

        def _pairwise_euclidean(a, b):
            aa = jnp.sum(a * a, axis=-1)[:, None]
            bb = jnp.sum(b * b, axis=-1)[None, :]
            ab = a @ b.T
            return jnp.sqrt(jnp.maximum(aa + bb - 2.0 * ab, 0.0))

        def _dtw_cost(D):
            row0 = jnp.cumsum(D[0])

            def row_step(prev_row, d_row):
                first = d_row[0] + prev_row[0]

                def col_step(left, inp):
                    d_ij, up, diag = inp
                    r = d_ij + jnp.minimum(jnp.minimum(up, left), diag)
                    return (r, r)
                _, rest = lax.scan(col_step, first, (d_row[1:], prev_row[1:], prev_row[:-1]))
                row = jnp.concatenate([first[None], rest])
                return (row, row)
            _, rows = lax.scan(row_step, row0, D[1:])
            return jnp.concatenate([row0[None], rows], axis=0)

        def _backtrack(R, T1, T2):
            L = T1 + T2 - 1

            def step(carry, _):
                i, j, done = carry
                valid = jnp.logical_not(done)
                cd = jnp.where((i > 0) & (j > 0), R[jnp.maximum(i - 1, 0), jnp.maximum(j - 1, 0)], BIG)
                cu = jnp.where(i > 0, R[jnp.maximum(i - 1, 0), j], BIG)
                cl = jnp.where(j > 0, R[i, jnp.maximum(j - 1, 0)], BIG)
                choice = jnp.argmin(jnp.stack([cd, cu, cl]))
                ni = jnp.where(choice <= 1, i - 1, i)
                nj = jnp.where((choice == 0) | (choice == 2), j - 1, j)
                at_origin = (i == 0) & (j == 0)
                ni = jnp.where(at_origin, 0, ni)
                nj = jnp.where(at_origin, 0, nj)
                return ((ni, nj, done | at_origin), (i, j, valid))
            init = (jnp.int32(T1 - 1), jnp.int32(T2 - 1), jnp.bool_(False))
            _, (i_idx, j_idx, valid) = lax.scan(step, init, None, length=L)
            return (i_idx, j_idx, valid)

        def _align_one(small, large):
            T_small, d = small.shape
            T_large = large.shape[0]
            D = _pairwise_euclidean(small, large)
            R = _dtw_cost(D)
            i_idx, j_idx, valid = _backtrack(R, T_small, T_large)
            contrib = small[i_idx] * valid[:, None].astype(small.dtype)
            expanded = jnp.zeros((T_large, d), dtype=small.dtype).at[j_idx].add(contrib)
            return expanded
        return jax.vmap(_align_one)(teacher_features, student_features)

    def _L0_ffn_ref(x, w1, b1, w2, b2):
        import jax, jax.numpy as jnp
        import numpy as np
        EPS = 1e-08

        def _ste(x, q):
            return x + jax.lax.stop_gradient(q - x)

        def quant_act_uint8(x):
            s = jax.lax.stop_gradient(jnp.maximum(jnp.max(x), EPS)) / 255.0
            q = jnp.clip(jnp.round(x / s), 0.0, 255.0) * s
            return (_ste(x, q), s)

        def quant_weight_int8_perchannel(w):
            s = jax.lax.stop_gradient(jnp.maximum(jnp.max(jnp.abs(w), axis=1, keepdims=True), EPS)) / 127.0
            q = jnp.clip(jnp.round(w / s), -128.0, 127.0) * s
            return (_ste(w, q), s[:, 0])

        def quant_bias_int32(b, s_in, s_w):
            s = jax.lax.stop_gradient(s_in * s_w)
            q = jnp.round(b / s) * s
            return _ste(b, q)

        def quant_linear(x, w, b):
            xq, s_in = quant_act_uint8(x)
            wq, s_w = quant_weight_int8_perchannel(w)
            bq = quant_bias_int32(b, s_in, s_w)
            return jnp.einsum('btd,fd->btf', xq, wq) + bq
        h = jax.nn.relu(quant_linear(x, w1, b1))
        return quant_linear(h, w2, b2)
    x = x + _L0_xattn_ref(ctx_1024, _layernorm(x, axis=-1))
    x = x + _L0_ffn_ref(_layernorm(x, axis=-1), L0_ffn_w1, L0_ffn_b1, L0_ffn_w2, L0_ffn_b2)
    return x

_drawn_inputs = setup_inputs


def setup_inputs(seed=0):
    import zlib

    import numpy as np

    out = dict(_drawn_inputs(seed))
    spreads = {}
    factors = {'L0_ffn_b1': 6.915, 'L0_ffn_b2': 7.978}
    for name, (base, spread) in spreads.items():
        noise = np.random.default_rng([zlib.crc32(name.encode()), seed]).standard_normal(out[name].shape)
        drawn = base * np.exp(spread * noise) if base else spread * noise
        out[name] = jnp.asarray(drawn.astype(out[name].dtype))
    for name, factor in factors.items():
        out[name] = (out[name] * factor).astype(out[name].dtype)
    return out
```

```python
import concourse.bass as bass
from concourse import mybir
from concourse.alu_op_type import AluOpType as ALU
from contextlib import ExitStack

ACT = mybir.ActivationFunctionType
AX = mybir.AxisListType.X
F32 = mybir.dt.float32
BF16 = mybir.dt.bfloat16

P = 128
B, S, D = 8, 512, 512
T = 77
FF = 2048
Q = S // P
K = D // P
NF = FF // P
NT = B * Q
BIG = 1.0e30
EPS_LN = 1.0e-5
EPS_Q = 1.0e-8
MAGIC = 12582912.0
TWO23 = 8388608.0

C = P // B
CW = S // C + 1
SK = T + C - 1
RW = CW + 1
LAST = S - 1 - (C - 1) * CW
PAD = C * CW

DIAG = 40.0
OUT = 128.0


def constants(np):
    p = np.arange(P)
    c = RW - np.arange(RW, dtype=np.float32)
    step = np.eye(P) + np.where((p[:, None] // C == p[None, :] // C) & (p[:, None] == p[None, :] + 1), 1 / OUT, 0)
    first = np.where(p % C == 0, 0, BIG)
    begin = np.where(p % C == C - 1, RW - 1 - LAST, 0)
    return {
        "identity": np.eye(P, dtype=np.float32),
        "walk_step": step.astype(np.float32),
        "codes": np.broadcast_to(np.concatenate([c, c + DIAG]), (P, 2 * RW)).astype(np.float32).copy(),
        "ends": np.stack([first, begin], 1).astype(np.float32),
    }


def build(nc, x, ctx_in, w1, b1, w2, b2, identity, walk_step, codes_in, ends_in, out):
    with ExitStack() as stack:
        def sb(name, shape, dt=F32):
            return stack.enter_context(nc.sbuf_tensor(name, shape, dt))

        def sem(name):
            return stack.enter_context(nc.semaphore(name))

        big = sb("big", [P, 4 * NF * S])
        xq_store = sb("xq_store", [P, NF * S])
        w1q_store = sb("w1q_store", [P, 2 * Q * S])
        w2q_store = sb("w2q_store", [P, 2 * Q * S])
        ctx_rows = sb("ctx_rows", [P, B, D])
        ybuf = sb("ybuf", [P, 4, 512])
        ident = sb("ident", [P, P])
        identb = sb("identb", [P, P], BF16)
        walk = sb("walk", [P, P], BF16)
        codes = sb("codes", [P, 2 * RW])
        ends = sb("ends", [P, 2])
        stats = sb("stats", [P, Q, 6])
        mv = sb("mv", [P, Q, 2])
        small = sb("small", [P, 8, Q])
        aa = sb("aa", [P, B])
        tiny = sb("tiny", [P, 1])
        magic = sb("magic", [P, 1])
        walked = sb("walked", [P, SK], BF16)
        wcodes = sb("wcodes", [P, 4, SK], BF16)
        span = sb("span", [P, 2, P])
        rmax = sb("rmax", [P, Q])
        ymax = sb("ymax", [P, NT + 4])
        wsc = sb("wsc", [P, 3, 20])
        bcol = sb("bcol", [P, NF])
        aff = sb("aff", [P, 6, NF])
        qrow = sb("qrow", [1, 8])
        qsc = sb("qsc", [P, 2, 2])
        onesr = sb("onesr", [1, P])
        hmax = sb("hmax", [P, B * 4])
        x2_dram = nc.dram_tensor("x2_dram", (B, P, Q, D), F32, kind="Internal").ap()
        h_dram = nc.dram_tensor("h_dram", (4, P, NF * S), F32, kind="Internal").ap()
        cost_dram = nc.dram_tensor("cost_dram", (B, C * (SK + 1) * CW), F32, kind="Internal").ap()
        s2_dram = nc.dram_tensor("s2_dram", (K, P), F32, kind="Internal").ap()

        half = 2 * NF * S
        X = big[:, 0:half].rearrange("p (b q d) -> p b q d", b=B, q=Q)
        Y2T = big[:, half:2 * half].rearrange("p (b k s) -> p b k s", b=B, k=K)
        H = big[:, :].rearrange("p (n f s) -> p n f s", n=4, f=NF)
        o = half
        R = big[:, o:o + (SK + 2) * RW]
        o += (SK + 2) * RW
        M = big[:, o:o + SK * RW]
        o += SK * RW
        COST = big[:, o:o + SK * CW]
        o += SK * CW
        L = big[:, o:o + SK * RW]
        o += SK * RW
        F = big[:, o:o + SK * RW]
        o += SK * RW
        assert o <= 2 * half
        ctxT = F[:, 0:K * B * T].rearrange("p (k n) -> p k n", k=K)
        dist = [z[:, 0:4 * PAD].rearrange("p (n s) -> p n s", n=4) for z in (R, M)]
        bbw = R[:, 4 * PAD:4 * PAD + 2 * Q * T].rearrange("p (n q i) -> p n q i", n=2, q=Q)
        tail = big[:, 2 * half - 2048:2 * half]
        spans = [tail[0:T, 264 * n:264 * n + 264].bitcast(BF16) for n in range(2)]
        path = [tail[0:T, 528 + 528 * n:528 + 528 * n + PAD] for n in range(2)]
        RAW = xq_store[:, :].rearrange("p (n s) -> p n s", n=NF)
        XQ = xq_store[:, :].bitcast(BF16).rearrange("p (b k s) -> p b k s", b=B, k=K)
        HQ = xq_store[:, :].bitcast(BF16).rearrange("p (n f s) -> p n f s", n=2, f=NF)
        Y = w1q_store[:, :].rearrange("p (n q d) -> p n q d", n=2, q=Q)
        YT = w2q_store[:, :].rearrange("p (n k s) -> p n k s", n=2, k=K)
        W1 = w1q_store[:, :].bitcast(BF16).rearrange("p (k f) -> p k f", k=K)
        W2 = w2q_store[:, :].bitcast(BF16).rearrange("p (f d) -> p f d", f=NF)
        XB = w1q_store[:, :].rearrange("p (n q d) -> p n q d", n=2, q=Q)
        s2row = ctx_rows[:, 0, :]
        b2row = ctx_rows[:, 1, :]
        brow = [ctx_rows[:, 2 + n, :] for n in range(6)]
        wqb = ybuf[:, :, :].rearrange("p n s -> p (n s)").bitcast(BF16).rearrange("p (n s) -> p n s", n=8)

        bank = [stack.enter_context(nc.psum_tensor(f"bank{n}", [P, 512], F32)) for n in range(8)]

        s_dve = sem("s_dve")
        s_const = sem("s_const")
        s_ctx = sem("s_ctx")
        s_x = [sem(f"s_xin{b}") for b in range(B)]
        s_raw = [sem(f"s_raw{n}") for n in range(3)]
        s_zero = sem("s_zero")
        s_gz = sem("s_gz")
        s_gw = [sem(f"s_gw{n}") for n in range(2)]
        s_cost = sem("s_cost")
        s_tiny = sem("s_tiny")
        s_wmax = sem("s_wmax")
        s_ctp = sem("s_ctp")
        s_ctc = sem("s_ctc")
        s_var = sem("s_var")
        s_sd = sem("s_sd")
        s_y = sem("s_y")
        s_ytp = sem("s_ytp")
        s_ytc = sem("s_ytc")
        s_bb = sem("s_bb")
        s_d = sem("s_d")
        s_d2 = sem("s_d2")
        s_s0 = sem("s_s0")
        s_rc = sem("s_rc")
        s_c = sem("s_c")
        s_v = sem("s_v")
        s_wt = sem("s_wt")
        s_wq = sem("s_wq")
        s_wtp = sem("s_wtp")
        s_wtc = sem("s_wtc")
        s_dp = sem("s_dp")
        s_look = sem("s_look")
        s_step = sem("s_step")
        s_dsk = sem("s_dsk")
        s_dskp = sem("s_dskp")
        s_ab = sem("s_ab")
        s_path = sem("s_path")
        s_ex = sem("s_ex")
        s_x2 = sem("s_x2")
        s_nb = sem("s_nb")
        s_y2 = sem("s_y2")
        s_y2p = sem("s_y2p")
        s_y2c = sem("s_y2c")
        s_spill = sem("s_spill")
        s_mx = sem("s_mx")
        s_mxp = sem("s_mxp")
        s_qr = sem("s_qr")
        s_qb = sem("s_qb")
        s_qs = sem("s_qs")
        s_xt = sem("s_xt")
        s_xq = sem("s_xq")
        s_aff = sem("s_aff")
        s_l1 = sem("s_l1")
        s_h = sem("s_h")
        s_hm = sem("s_hm")
        s_hsp = [sem(f"s_hsp{n}") for n in range(4)]
        s_hre = [sem(f"s_hre{n}") for n in range(4)]
        s_ht = sem("s_ht")
        s_hq = sem("s_hq")
        s_xb = [sem(f"s_xb{n}") for n in range(2)]
        s_xbb = sem("s_xbb")
        s_l2 = sem("s_l2")
        s_o = sem("s_o")
        s_sum = sem("s_sum")
        s_out = [sem(f"s_out{n}") for n in range(2)]
        s_s2w = sem("s_s2w")
        s_s2r = sem("s_s2r")
        s_b1 = sem("s_b1")
        s_rows = sem("s_rows")

        block = stack.enter_context(nc.Block())

        x_v = x.rearrange("b (q p) d -> b p q d", p=P)
        out_v = out.rearrange("b (q p) d -> b p q d", p=P)
        w1_v = w1.rearrange("(n p) d -> p n d", p=P)
        w2_v = w2.rearrange("(n p) (h f) -> p n h f", p=P, h=4)
        order = [4, 5, 6, 7, 0, 1, 2, 3]

        @block.sync
        def _(sp):
            sp.dma_start(ctx_rows[0:T, :, :], ctx_in.rearrange("b i d -> i b d")).then_inc(s_ctx, 16)
            for dst, src in ((ident[:, :], identity), (ybuf[:, 0, 0:P], walk_step), (codes[:, :], codes_in),
                             (ends[:, :], ends_in)):
                sp.dma_start(dst, src).then_inc(s_const, 16)
            sp.dma_start(X[:, 0, :, :], x_v[0]).then_inc(s_x[0], 16)
            sp.dma_start(RAW.rearrange("p (n h) s -> p n h s", n=4), w2_v).then_inc(s_raw[0], 16)
            for b in range(1, 4):
                sp.dma_start(X[:, b, :, :], x_v[b]).then_inc(s_x[b], 16)
            sp.wait_ge(s_wmax, 1)
            sp.dma_start(RAW, w1_v).then_inc(s_raw[1], 16)
            for b in range(4, B):
                sp.dma_start(X[:, b, :, :], x_v[b]).then_inc(s_x[b], 16)
            with nc.allow_non_contiguous_dma(reason="2048 words, off the critical path"):
                sp.dma_start(bcol[:, :], b1.rearrange("(n p) -> p n", p=P)).then_inc(s_b1, 16)
            sp.wait_ge(s_zero, 1)
            for b in range(B):
                sp.dma_start(cost_dram[b, 0:C * SK * CW].rearrange("(c t) -> c t", c=C),
                             COST[C * b:C * b + C, :]).then_inc(s_gz, 16)
            sp.dma_start(cost_dram[:, C * SK * CW:].rearrange("b (o n) -> (b o) n", o=1),
                         COST[0:B, 0:C * CW]).then_inc(s_gz, 16)
            sp.wait_ge(s_gz, 16 * (B + 1))
            for b in range(B):
                sp.wait_ge(s_c, b + 1)
                skewed = cost_dram[b].rearrange("(c z) -> c z", c=C)[:, 0:T * CW]
                sp.dma_start(skewed.rearrange("c (i j) -> i c j", j=CW),
                             dist[b % 2][0:T, 3, :].rearrange("i (c j) -> i c j", j=CW)).then_inc(s_gw[b % 2], 16)
            for n in range(2):
                sp.wait_ge(s_gw[n], 16 * B // 2)
            for b in range(B):
                sp.dma_start(COST[C * b:C * b + C, :],
                             cost_dram[b, 0:C * SK * CW].rearrange("(c t) -> c t", c=C)).then_inc(s_cost, 16)
            sp.wait_ge(s_wq, NF)
            sp.dma_start(RAW.rearrange("p (n h) s -> p n h s", n=4), w2_v).then_inc(s_raw[2], 16)
            for b in range(B):
                sp.wait_ge(s_x2, (b + 1) * Q)
                sp.dma_start(x2_dram[b], X[:, b, :, :]).then_inc(s_spill, 16)
            sp.wait_ge(s_s2w, 16)
            sp.wait_ge(s_ex, B * Q)
            sp.dma_start(s2row, s2_dram.rearrange("n (o p) -> o (n p)", o=1).broadcast_to([P, D])).then_inc(s_s2r, 16)
            sp.dma_start(brow[0], b2.rearrange("(o n) -> o n", o=1).broadcast_to([P, D])).then_inc(s_s2r, 16)
            for n in range(4):
                for g in range(4):
                    sp.wait_ge(s_h, n * NF + 4 * g + 4)
                    sp.dma_start(h_dram[n, :, g * 2048:g * 2048 + 2048],
                                 H[:, n, 4 * g:4 * g + 4, :]).then_inc(s_hsp[n], 16)
            for i in range(B):
                if i == 0:
                    sp.wait_ge(s_spill, 16 * B)
                    sp.wait_ge(s_l1, B * NF)
                if i >= 2:
                    sp.wait_ge(s_out[i % 2], 16 * (i // 2))
                sp.dma_start(XB[:, i % 2, :, :], x2_dram[order[i]]).then_inc(s_xb[i % 2], 16)
                if i < 4:
                    for g in range(4):
                        sp.wait_ge(s_hq, 4 * i + g + 1)
                        if g == 0:
                            sp.wait_ge(s_hsp[i], 64)
                        sp.dma_start(H[:, i, 4 * g:4 * g + 4, :],
                                     h_dram[i, :, g * 2048:g * 2048 + 2048]).then_inc(s_hre[i], 16)
                if i >= 1:
                    sp.wait_ge(s_sum, Q * i)
                    sp.dma_start(out_v[order[i - 1]], XB[:, (i - 1) % 2, :, :]).then_inc(s_out[(i - 1) % 2], 16)
            sp.wait_ge(s_sum, Q * B)
            sp.dma_start(out_v[order[B - 1]], XB[:, (B - 1) % 2, :, :]).then_inc(s_out[(B - 1) % 2], 16)
            sp.wait_ge(s_out[0], 16 * B // 2)
            sp.wait_ge(s_out[1], 16 * B // 2)

        @block.gpsimd
        def _(pool):
            g = nc.gpsimd
            g.memset(COST, 0.0).then_inc(s_zero, 1)
            g.memset(tiny[:, :], 1e-30).then_inc(s_tiny, 1)
            g.memset(onesr[:, :], 1.0).then_inc(s_tiny, 1)
            g.memset(magic[:, :], MAGIC).then_inc(s_tiny, 1)
            for n in range(2):
                g.memset(dist[n][0:T, 3, S:PAD], BIG).then_inc(s_tiny, 1)
            pool.wait_ge(s_const, 64)
            g.tensor_copy(identb[:, :], ident[:, :]).then_inc(s_tiny, 1)
            g.tensor_copy(walk[:, :], ybuf[:, 0, 0:P]).then_inc(s_tiny, 1)
            pool.wait_ge(s_tiny, 7)
            for b in range(B):
                t = dist[b % 2][0:T]
                pool.wait_ge(s_rc, b + 1)
                g.tensor_tensor(t[:, 2, 0:S], t[:, 0, 0:S], t[:, 2, 0:S], ALU.mult).then_inc(s_v, 1)
                pool.wait_ge(s_v, b + 1)
                if b >= 2:
                    pool.wait_ge(s_gw[b % 2], 16 * (b // 2))
                g.tensor_tensor(t[:, 3, 0:S], t[:, 1, 0:S], t[:, 2, 0:S], ALU.add).then_inc(s_c, 1)
            for n in range(2 * NF):
                pool.wait_ge(s_wt, n + 1)
                if n >= 8:
                    pool.wait_ge(s_wtp, n - 7)
                g.tensor_scalar(wqb[:, n % 8, :], RAW[:, n % NF, :], MAGIC, 127.0, ALU.subtract,
                                ALU.min).then_inc(s_wq, 1)
            for b in range(B):
                pool.wait_ge(s_ab, b + 1)
                if b >= 2:
                    pool.wait_ge(s_ex, Q * (b - 1))
                g.tensor_tensor(path[b % 2], spans[0], spans[1], ALU.mult).then_inc(s_path, 1)
            pool.wait_ge(s_rows, 1)
            for i in range(B):
                pool.wait_ge(s_xb[i % 2], 16 * (i // 2 + 1))
                for q in range(Q):
                    g.tensor_tensor(XB[:, i % 2, q, :], XB[:, i % 2, q, :], b2row, ALU.add).then_inc(s_xbb, 1)
                for q in range(Q):
                    n = i * Q + q
                    pool.wait_ge(s_xbb, n + 1)
                    pool.wait_ge(s_o, n + 1)
                    g.tensor_tensor(XB[:, i % 2, q, :], XB[:, i % 2, q, :], ybuf[:, q, :], ALU.add).then_inc(s_sum, 1)

        @block.scalar
        def _(act):
            a = nc.scalar
            ID = ACT.Identity
            for n in range(2 * K):
                act.wait_ge(s_ctp, n + 1)
                k, h = n // 2, n % 2
                a.activation(ctxT[:, k, 4 * T * h:4 * T * h + 4 * T], bank[n % 4][:, 0:4 * T], ID).then_inc(s_ctc, 1)

            def roots(b):
                act.wait_ge(s_var, b + 1)
                a.activation(small[:, 1, :], small[:, 0, :], ACT.Sqrt).then_inc(s_sd, 1)

            def costs(b):
                t = dist[b % 2][0:T]
                act.wait_ge(s_d, b + 1)
                if b >= 2:
                    act.wait_ge(s_c, b - 1)
                a.activation(t[:, 0, 0:S], bank[4 + b % 2][0:T, :], ACT.Relu, bias=aa[0:T, b:b + 1],
                             scale=-2.0).then_inc(s_d2, 1)
                act.wait_ge(s_d2, b + 1)
                a.activation(t[:, 1, 0:S], t[:, 0, 0:S], ACT.Sqrt, bias=tiny[0:T, :]).then_inc(s_s0, 1)

            act.wait_ge(s_tiny, 7)
            act.wait_ge(s_bb, B)
            roots(0)
            for b in range(B):
                if b >= 2:
                    act.wait_ge(s_d, b - 1)
                for k in range(K):
                    act.wait_ge(s_ytp, b * K + k + 1)
                    a.activation(YT[:, b % 2, k, :], bank[k][:, :], ID).then_inc(s_ytc, 1)
                if b + 1 < B:
                    roots(b + 1)
                if b >= 1:
                    costs(b - 1)
            costs(B - 1)

            for n in range(2 * NF + 2):
                if n < 2 * NF:
                    if n == 0:
                        act.wait_ge(s_wmax, 3)
                    if n == NF:
                        act.wait_ge(s_raw[2], 16)
                    col = n if n < NF else NF + (n - NF) // 4
                    a.activation(RAW[:, n % NF, :], RAW[:, n % NF, :], ID, bias=magic[:, :],
                                 scale=wsc[:, 2, col:col + 1]).then_inc(s_wt, 1)
                m = n - 2
                if m >= 0:
                    act.wait_ge(s_wtp, m + 1)
                    src = bank[m % 2][:, 0:256].bitcast(BF16).rearrange("p (k f) -> p k f", k=4)
                    if m < NF:
                        dst = W1[:, :, m * P:m * P + P]
                    else:
                        dt_, h = (m - NF) // 4, (m - NF) % 4
                        dst = W2[:, 4 * h:4 * h + 4, dt_ * P:dt_ * P + P]
                    a.activation(dst, src, ID).then_inc(s_wtc, 1)

            with nc.allow_non_contiguous_dma(reason="512 words, off the critical path"):
                act.dma_start(s2_dram.rearrange("n p -> p n"), wsc[:, 1, NF:NF + 4]).then_inc(s_s2w, 16)

            for b in range(B):
                act.wait_ge(s_var, B + b + 1)
                a.activation(small[:, 1, :], small[:, 0, :], ACT.Sqrt).then_inc(s_sd, 1)
                act.wait_ge(s_nb, b + 1)
                if b >= 1:
                    act.wait_ge(s_y2p, K * b)
                for q in range(Q):
                    a.activation(ybuf[:, q, :], X[:, b, q, :], ID, bias=small[:, 6, q:q + 1],
                                 scale=small[:, 5, q:q + 1]).then_inc(s_y2, 1)
                for k in range(K):
                    act.wait_ge(s_y2p, b * K + k + 1)
                    a.activation(Y2T[:, b, k, :], bank[k][:, :], ID).then_inc(s_y2c, 1)

            def tokens_up(b):
                a.activation(Y2T[:, b, :, :], Y2T[:, b, :, :], ID, bias=magic[:, :],
                             scale=qsc[:, 0, 1:2]).then_inc(s_xt, 1)

            act.wait_ge(s_qs, 1)
            act.wait_ge(s_y2c, B * K)
            for b in range(B):
                tokens_up(b)
            act.wait_ge(s_aff, 1)
            act.wait_ge(s_spill, 16 * B)
            for n in range(B):
                if n == 2:
                    act.wait_ge(s_xq, B)
                for f in range(NF):
                    if n >= 4 and f == 0:
                        act.wait_ge(s_hsp[n - 4], 64)
                    act.wait_ge(s_l1, n * NF + f + 1)
                    if n >= 4 and f % 4 == 0:
                        act.wait_ge(s_hm, (n - 4) * 4 + f // 4 + 1)
                    a.activation(H[:, n % 4, f, :], bank[f % 8][:, :], ACT.Relu, bias=aff[:, 1, f:f + 1],
                                 scale=aff[:, 0, f:f + 1]).then_inc(s_h, 1)
            act.wait_ge(s_qs, 2)
            for i in range(B):
                for g in range(4):
                    if i >= 4:
                        act.wait_ge(s_hre[i - 4], 64)
                    a.activation(H[:, i % 4, 4 * g:4 * g + 4, :], H[:, i % 4, 4 * g:4 * g + 4, :], ID,
                                 bias=magic[:, :], scale=qsc[:, 1, 1:2]).then_inc(s_ht, 1)

        @block.vector
        def _(dve):
            v = nc.vector
            chain = [0]

            def link(ins):
                chain[0] += 1
                ins.then_inc(s_dve, 1)
                dve.wait_ge(s_dve, chain[0])

            def scales(at, n):
                link(v.tensor_scalar(wsc[:, 1, at:at + n], wsc[:, 0, at:at + n], EPS_Q, 1.0 / 127.0, ALU.max, ALU.mult))
                v.reciprocal(wsc[:, 2, at:at + n], wsc[:, 1, at:at + n]).then_inc(s_wmax, 1)

            def moments(b, src, last):
                for q in range(Q):
                    v.bn_stats(stats[:, q, :], src[:, q, :]).then_inc(s_dve, 1)
                chain[0] += Q
                dve.wait_ge(s_dve, chain[0])
                for q in range(Q):
                    v.bn_aggr(mv[:, q, :], stats[:, q, :]).then_inc(s_dve, 1)
                chain[0] += Q
                dve.wait_ge(s_dve, chain[0])
                v.tensor_scalar(small[:, 0, :], mv[:, :, 1], EPS_LN, None, ALU.add).then_inc(s_var, 1)
                dve.wait_ge(s_sd, last)
                link(v.reciprocal(small[:, 2, :], small[:, 1, :]))
                link(v.tensor_tensor(small[:, 3, :], small[:, 2, :], small[:, 2, :], ALU.mult))
                link(v.tensor_tensor(small[:, 3, :], small[:, 3, :], small[:, 0, :], ALU.mult))
                link(v.tensor_scalar(small[:, 3, :], small[:, 3, :], -0.5, 1.5, ALU.mult, ALU.add))

            dve.wait_ge(s_ctx, 16)
            for b in range(B):
                if b >= 2:
                    dve.wait_ge(s_bb, b - 1)
                v.tensor_tensor_reduce(dist[0][0:T, b % 2, 0:S], ctx_rows[0:T, b, :], ctx_rows[0:T, b, :], 1.0, 0.0,
                                       ALU.mult, ALU.add, aa[0:T, b:b + 1]).then_inc(s_bb, 1)

            def weights_max(n):
                dve.wait_ge(s_raw[n], 16)
                if n == 0:
                    link(v.tensor_reduce(wsc[:, 0, NF:NF + 4], RAW.rearrange("p (n h) s -> p n (h s)", n=4), AX,
                                         ALU.max, apply_absolute_value=True))
                    scales(NF, 4)
                else:
                    link(v.tensor_reduce(wsc[:, 0, 0:NF], RAW, AX, ALU.max, apply_absolute_value=True))
                    scales(0, NF)

            def after_costs(b):
                t = dist[b % 2][0:T]
                dve.wait_ge(s_s0, b + 1)
                v.reciprocal(t[:, 2, 0:S], t[:, 1, 0:S]).then_inc(s_rc, 1)

            for b in range(B):
                dve.wait_ge(s_x[b], 16)
                moments(b, X[:, b, :, :], b + 1)
                link(v.tensor_tensor(small[:, 5, :], small[:, 2, :], small[:, 3, :], ALU.mult))
                link(v.tensor_tensor(small[:, 4, :], small[:, 5, :], small[:, 5, :], ALU.mult))
                link(v.tensor_tensor(small[:, 4, :], small[:, 4, :], mv[:, :, 1], ALU.mult))
                if b >= 2:
                    dve.wait_ge(s_d, b - 1)
                v.tensor_scalar(bbw[:, b % 2, :, :], small[:, 4, :].unsqueeze(2).broadcast_to([P, Q, T]), -0.5 * D,
                                None, ALU.mult).then_inc(s_bb, 1)
                if b >= 2:
                    dve.wait_ge(s_ytp, K * (b - 1))
                for q in range(Q):
                    v.tensor_scalar(Y[:, b % 2, q, :], X[:, b, q, :], mv[:, q, 0:1], small[:, 5, q:q + 1],
                                    ALU.subtract, ALU.mult).then_inc(s_y, 1)
                dve.wait_ge(s_y, Q * (b + 1))
                if b == 1:
                    weights_max(0)
                if b == 5:
                    weights_max(1)
                if b >= 2:
                    after_costs(b - 2)
            after_costs(B - 2)
            after_costs(B - 1)
            v.memset(wsc[:, 0, 0:1], 0.0).then_inc(s_wmax, 1)

            def row(t, a, n):
                return R[:, t * RW + a:t * RW + a + n]

            left = [C * (i // C) + (i % C - 1) % C for i in range(32)]
            for n in range(2):
                dve.wait_ge(s_gw[n], 16 * B // 2)
            link(v.memset(R[:, 0:2 * RW], BIG))
            link(v.tensor_copy(R[:, 0:1], ends[:, 0:1]))
            v.memset(L, 0.0).then_inc(s_dve, 1)
            v.memset(F, OUT).then_inc(s_dve, 1)
            chain[0] += 2
            v.tensor_tensor(M[:, 0:CW], row(0, 1, CW), row(0, 0, CW), ALU.min).then_inc(s_dp, 1)
            dve.wait_ge(s_cost, 16 * B)
            for t in range(SK):
                dve.wait_ge(s_dp, 1 + 3 * t)
                v.tensor_tensor_scan(row(t + 1, 1, CW), M[:, t * CW:t * CW + CW], COST[:, t * CW:t * CW + CW],
                                     row(t + 1, 0, 1), ALU.min, ALU.add).then_inc(s_dp, 1)
                dve.wait_ge(s_dp, 2 + 3 * t)
                if t + 1 < SK:
                    v.tensor_tensor(M[:, (t + 1) * CW:(t + 2) * CW], row(t + 1, 1, CW), row(t + 1, 0, CW),
                                    ALU.min).then_inc(s_dp, 1)
                    v.stream_shuffle(row(t + 2, 0, 1), row(t + 1, CW, 1), left).then_inc(s_dp, 1)
            dve.wait_ge(s_dp, 2 + 3 * (SK - 1))
            dve.wait_ge(s_dve, chain[0])

            R3 = R.rearrange("p (t j) -> p t j", j=RW)
            M3 = M[:, 0:SK * CW].rearrange("p (t j) -> p t j", j=CW)
            L3 = L.rearrange("p (t j) -> p t j", j=RW)
            F3 = F.rearrange("p (t j) -> p t j", j=RW)
            v.tensor_tensor(L3[:, :, 1:RW], R3[:, 1:SK + 1, 0:CW], M3, ALU.is_lt).then_inc(s_dve, 1)
            v.tensor_tensor(F3[:, :, 1:RW], R3[:, 0:SK, 0:CW], R3[:, 0:SK, 1:RW], ALU.is_le).then_inc(s_dve, 1)
            chain[0] += 2
            dve.wait_ge(s_dve, chain[0])
            link(v.scalar_tensor_tensor(out=F3[:, :, 1:RW], in0=F3[:, :, 1:RW], scalar=DIAG + 1,
                                        in1=codes[:, 1:RW].unsqueeze(1).broadcast_to([P, SK, CW]),
                                        op0=ALU.mult, op1=ALU.add))
            link(v.scalar_tensor_tensor(out=F3[:, :, 1:RW], in0=L3[:, :, 1:RW], scalar=0.0, in1=F3[:, :, 1:RW],
                                        op0=ALU.is_equal, op1=ALU.mult))
            link(v.tensor_tensor_scan(M, L, F, OUT, ALU.mult, ALU.add))

            N3 = M.rearrange("p (t j) -> p t j", j=RW)
            both = codes[:, :].rearrange("p (n j) -> p n j", n=2)
            junk = F[:, 0:2 * RW].rearrange("p (n j) -> p n j", n=2)
            for n in range(SK):
                t = SK - 1 - n
                if n:
                    dve.wait_ge(s_step, n)
                at = ends[:, 1:2] if n == 0 else bank[6][:, t:t + 1]
                v.scalar_tensor_tensor(out=junk, in0=both, scalar=at,
                                       in1=N3[:, t, :].unsqueeze(1).broadcast_to([P, 2, RW]), op0=ALU.is_equal,
                                       op1=ALU.mult, accum_out=walked[:, t:t + 1]).then_inc(s_look, 1)
            dve.wait_ge(s_look, SK)
            link(v.tensor_copy(wcodes[:, 0, SK - 1:SK], ends[:, 1:2]))
            link(v.tensor_copy(wcodes[:, 0, 0:SK - 1], bank[6][:, 0:SK - 1]))
            link(v.tensor_scalar(wcodes[:, 1, :], wcodes[:, 0, :], DIAG + 0.5, -DIAG, ALU.is_ge, ALU.mult))
            link(v.tensor_tensor(wcodes[:, 2, :], wcodes[:, 0, :], wcodes[:, 1, :], ALU.add))
            link(v.tensor_scalar(wcodes[:, 1, :], walked[:, :], DIAG + 0.5, -DIAG - 1, ALU.is_ge, ALU.mult))
            v.tensor_tensor(wcodes[:, 3, :], walked[:, :], wcodes[:, 1, :], ALU.add).then_inc(s_dsk, 1)
            dve.wait_ge(s_dskp, 1)
            link(v.tensor_copy(span[0:T, :, :], bank[7][0:T, 0:2 * P].rearrange("p (n c) -> p n c", n=2)))

            def on_path(b):
                c3 = codes[0:T, 1:RW].unsqueeze(1).broadcast_to([T, C, CW])
                sp3 = span[0:T, :, :].rearrange("p n (c b) -> p n b c", b=B)
                if b >= 1:
                    dve.wait_ge(s_path, b)
                for n, op in ((0, ALU.is_ge), (1, ALU.is_le)):
                    ins = v.tensor_tensor(spans[n].rearrange("p (c j) -> p c j", c=C), c3,
                                          sp3[:, n, b, :].unsqueeze(2).broadcast_to([T, C, CW]), op)
                ins.then_inc(s_ab, 1)

            on_path(0)
            for b in range(B):
                if b + 1 < B:
                    on_path(b + 1)
                for q in range(Q):
                    n = b * Q + q
                    dve.wait_ge(s_ex, n + 1)
                    v.tensor_tensor_reduce(X[:, b, q, :], bank[4 + n % 4][:, :], X[:, b, q, :], 1.0, -3.0e38, ALU.add,
                                           ALU.max, rmax[:, q:q + 1]).then_inc(s_x2, 1)
                dve.wait_ge(s_x2, Q * (b + 1))
                if b >= 1:
                    dve.wait_ge(s_y2, Q * b)
                moments(b, X[:, b, :, :], B + b + 1)
                link(v.tensor_tensor(small[:, 5, :], small[:, 2, :], small[:, 3, :], ALU.mult))
                v.scalar_tensor_tensor(out=small[:, 6, :], in0=mv[:, :, 0], scalar=-1.0, in1=small[:, 5, :],
                                       op0=ALU.mult, op1=ALU.mult).then_inc(s_nb, 1)
                link(v.tensor_tensor(small[:, 4, :], rmax[:, :], mv[:, :, 0], ALU.subtract))
                link(v.tensor_tensor(ymax[:, b * Q:b * Q + Q], small[:, 4, :], small[:, 5, :], ALU.mult))

            def step_size(n, src):
                v.tensor_reduce(ymax[:, NT + n:NT + n + 1], src, AX, ALU.max).then_inc(s_mx, 1)
                dve.wait_ge(s_mxp, n + 1)
                link(v.tensor_reduce(qrow[:, 0:1], bank[7][0:1, 0:P], AX, ALU.max))
                link(v.tensor_scalar(qrow[:, 1:2], qrow[:, 0:1], EPS_Q, 1.0 / 255.0, ALU.max, ALU.mult))
                v.reciprocal(qrow[:, 2:3], qrow[:, 1:2]).then_inc(s_qr, 1)
                dve.wait_ge(s_qb, n + 1)
                v.tensor_copy(qsc[:, n, :], bank[6][:, 0:2]).then_inc(s_qs, 1)
                dve.wait_ge(s_qs, n + 1)

            def on_grid(dst, bias, scale, t):
                link(v.reciprocal(t[0], scale))
                link(v.tensor_tensor(t[0], bias, t[0], ALU.mult))
                link(v.scalar_tensor_tensor(out=t[1], in0=t[0], scalar=-1.0, in1=t[0], op0=ALU.mult, op1=ALU.max))
                link(v.tensor_scalar(t[2], t[1], TWO23, TWO23, ALU.add, ALU.subtract))
                link(v.tensor_tensor(t[3], t[1], t[2], ALU.subtract))
                link(v.scalar_tensor_tensor(out=t[3], in0=t[1], scalar=TWO23, in1=t[3], op0=ALU.is_ge, op1=ALU.mult))
                link(v.tensor_tensor(t[2], t[2], t[3], ALU.add))
                link(v.tensor_scalar(t[0], t[0], 0.0, 2.0, ALU.is_ge, ALU.mult))
                link(v.scalar_tensor_tensor(out=t[2], in0=t[0], scalar=-1.0, in1=t[2], op0=ALU.add, op1=ALU.mult))
                v.tensor_tensor(dst, t[2], scale, ALU.mult).then_inc(s_aff if dst is not b2row else s_rows, 1)

            step_size(0, ymax[:, 0:NT])

            def tokens_down(b):
                dve.wait_ge(s_xt, b + 1)
                v.tensor_scalar(XQ[:, b, :, :], Y2T[:, b, :, :], MAGIC, 0.0, ALU.subtract, ALU.max).then_inc(s_xq, 1)

            dve.wait_ge(s_wtp, 2 * NF)
            tokens_down(0)
            link(v.tensor_scalar(aff[:, 0, :], wsc[:, 1, 0:NF], qsc[:, 0, 0:1], None, ALU.mult))
            dve.wait_ge(s_b1, 16)
            on_grid(aff[:, 1, :], bcol[:, :], aff[:, 0, :], [aff[:, 2 + i, :] for i in range(4)])
            for b in range(1, B):
                tokens_down(b)
            for n in range(B * 4):
                dve.wait_ge(s_h, 4 * n + 4)
                tb, g = n // 4, n % 4
                v.tensor_reduce(hmax[:, n:n + 1], H[:, tb % 4, 4 * g:4 * g + 4, :].rearrange("p f s -> p (f s)"), AX,
                                ALU.max).then_inc(s_hm, 1)
            dve.wait_ge(s_hm, B * 4)
            step_size(1, hmax[:, :])
            dve.wait_ge(s_s2r, 32)

            def hidden(i):
                for g in range(4):
                    dve.wait_ge(s_ht, 4 * i + g + 1)
                    if i >= 2 and g == 0:
                        dve.wait_ge(s_l2, Q * (i - 1))
                    v.tensor_scalar(HQ[:, i % 2, 4 * g:4 * g + 4, :], H[:, i % 4, 4 * g:4 * g + 4, :], MAGIC, 255.0,
                                    ALU.subtract, ALU.min).then_inc(s_hq, 1)

            hidden(0)
            link(v.tensor_scalar(s2row, s2row, qsc[:, 1, 0:1], None, ALU.mult))
            on_grid(b2row, brow[0], s2row, brow[1:5])
            for i in range(B):
                if i + 1 < B:
                    hidden(i + 1)
                for q in range(Q):
                    n = i * Q + q
                    dve.wait_ge(s_l2, n + 1)
                    if n >= 4:
                        dve.wait_ge(s_sum, n - 3)
                    v.tensor_tensor(ybuf[:, q, :], bank[n % 4][:, :], s2row, ALU.mult).then_inc(s_o, 1)

        @block.tensor
        def _(pe):
            t = nc.tensor
            pe.wait_ge(s_ctx, 16)
            pe.wait_ge(s_const, 64)
            for n in range(2 * K):
                k, h = n // 2, n % 2
                if n >= 4:
                    pe.wait_ge(s_ctc, n - 3)
                for j in range(4):
                    last = t.transpose(bank[n % 4][:, T * j:T * j + T],
                                       ctx_rows[0:T, 4 * h + j, k * P:k * P + P], ident[0:T, 0:T])
                last.then_inc(s_ctp, 1)

            def turn(b):
                for k in range(K):
                    if b == 0 and k == 0:
                        pe.wait_ge(s_ctc, 2 * K)
                    if b >= 1:
                        pe.wait_ge(s_ytc, (b - 1) * K + k + 1)
                    for q in range(Q):
                        if k == 0:
                            pe.wait_ge(s_y, b * Q + q + 1)
                        last = t.transpose(bank[k][:, q * P:q * P + P], Y[:, b % 2, q, k * P:k * P + P], ident[:, :])
                    last.then_inc(s_ytp, 1)

            def distances(b):
                d = bank[4 + b % 2][0:T, :]
                pe.wait_ge(s_ytc, (b + 1) * K)
                if b >= 2:
                    pe.wait_ge(s_d2, b - 1)
                pe.wait_ge(s_bb, B + b + 1)
                for k in range(K):
                    t.matmul(d, ctxT[:, k, b * T:b * T + T], YT[:, b % 2, k, :], start=(k == 0), stop=False)
                for q in range(Q):
                    last = t.matmul(d[:, q * P:q * P + P], bbw[:, b % 2, q, :], ident[:, :], start=False,
                                    stop=(q == Q - 1))
                last.then_inc(s_d, 1)

            for b in range(B):
                turn(b)
                if b >= 1:
                    distances(b - 1)
            distances(B - 1)

            for n in range(2 * NF):
                pe.wait_ge(s_wq, n + 1)
                if n == 0:
                    pe.wait_ge(s_ytc, B * K)
                if n >= 2:
                    pe.wait_ge(s_wtc, n - 1)
                dst = bank[n % 2][:, 0:256].bitcast(BF16)
                for k in range(4):
                    last = t.transpose(dst[:, k * P:k * P + P], wqb[:, n % 8, k * P:k * P + P], identb[:, :])
                last.then_inc(s_wtp, 1)

            for n in range(SK - 1):
                c = SK - 1 - n
                pe.wait_ge(s_look, n + 1)
                t.matmul(bank[6][:, c - 1:c], walk[:, :], walked[:, c:c + 1], start=True, stop=True).then_inc(s_step, 1)

            pe.wait_ge(s_dsk, 1)
            for n in range(2):
                for c in range(C):
                    last = t.matmul(bank[7][0:T, n * P + c * B:n * P + c * B + B], wcodes[:, 2 + n, c:c + T],
                                    identb[:, c:c + C * (B - 1) + 1:C], start=True, stop=True)
            last.then_inc(s_dskp, 1)

            def gather(b):
                pe.wait_ge(s_path, b + 1)
                for q in range(Q):
                    n = b * Q + q
                    if n == 0:
                        pe.wait_ge(s_d2, B)
                    if n >= 2:
                        pe.wait_ge(s_x2, n - 1)
                    t.matmul(bank[4 + n % 4][:, :], path[b % 2][:, q * P:q * P + P], ctx_rows[0:T, b, :],
                             start=True, stop=True).then_inc(s_ex, 1)

            def turn2(b):
                for k in range(K):
                    if b == 0 and k == 0:
                        pe.wait_ge(s_wtc, 2 * NF)
                    if b >= 1:
                        pe.wait_ge(s_y2c, (b - 1) * K + k + 1)
                    for q in range(Q):
                        if k == 0:
                            pe.wait_ge(s_y2, b * Q + q + 1)
                        last = t.transpose(bank[k][:, q * P:q * P + P], ybuf[:, q, k * P:k * P + P], ident[:, :])
                    last.then_inc(s_y2p, 1)

            gather(0)
            for b in range(B):
                if b + 1 < B:
                    gather(b + 1)
                turn2(b)

            def spread(n):
                pe.wait_ge(s_mx, n + 1)
                t.transpose(bank[7][0:1, 0:P], ymax[:, NT + n:NT + n + 1], ident[:, :]).then_inc(s_mxp, 1)
                pe.wait_ge(s_qr, n + 1)
                t.matmul(bank[6][:, 0:2], onesr[:, :], qrow[:, 1:3], start=True, stop=True).then_inc(s_qb, 1)

            pe.wait_ge(s_x2, B * Q)
            spread(0)
            pe.wait_ge(s_qs, 1)
            pe.wait_ge(s_y2c, B * K)
            for b in range(B):
                pe.wait_ge(s_xq, b + 1)
                for f in range(NF):
                    n = b * NF + f
                    if n >= 8:
                        pe.wait_ge(s_h, n - 7)
                    for k in range(K):
                        last = t.matmul(bank[f % 8][:, :], W1[:, k, f * P:f * P + P], XQ[:, b, k, :],
                                        start=(k == 0), stop=(k == K - 1))
                    last.then_inc(s_l1, 1)
            pe.wait_ge(s_h, B * NF)
            spread(1)
            for i in range(B):
                for q in range(Q):
                    n = i * Q + q
                    if n >= 4:
                        pe.wait_ge(s_o, n - 3)
                    for f in range(NF):
                        if q == 0 and f % 4 == 0:
                            pe.wait_ge(s_hq, 4 * i + f // 4 + 1)
                        last = t.matmul(bank[n % 4][:, :], HQ[:, i % 2, f, q * P:q * P + P], W2[:, f, :],
                                        start=(f == 0), stop=(f == NF - 1))
                    last.then_inc(s_l2, 1)


_INS = ["x", "ctx_1024", "L0_ffn_w1", "L0_ffn_b1", "L0_ffn_w2", "L0_ffn_b2"]


def kernel(**inputs):
    import numpy as np
    import concourse.bacc as bacc
    from concourse.bass_utils import run_bass_kernel_spmd as run

    nc = bacc.Bacc("TRN2", target_bir_lowering=False, num_devices=1, dynamic_dma_scratch_size=1024)
    arrays, args = {}, []
    for name in _INS:
        arrays[f"in_{name}"] = np.ascontiguousarray(inputs[name])
    for name, a in constants(np).items():
        arrays[f"const_{name}"] = a
    for name, a in arrays.items():
        args.append(nc.dram_tensor(name, a.shape, mybir.dt.from_np(a.dtype), kind="ExternalInput").ap())
    out = nc.dram_tensor("out_0", (B, S, D), F32, kind="ExternalOutput").ap()
    build(nc, *args, out)
    r = run(nc, [arrays], core_ids=[0])
    return r.results[0]["out_0"]
```

```python
import concourse.bass as bass
from concourse import mybir
from concourse.alu_op_type import AluOpType as ALU
from contextlib import ExitStack

ACT = mybir.ActivationFunctionType
AX = mybir.AxisListType.X
F32 = mybir.dt.float32
BF16 = mybir.dt.bfloat16

P = 128
B, S, D = 8, 512, 512
T = 77
FF = 2048
Q = S // P
K = D // P
NF = FF // P
NT = B * Q
BIG = 1.0e30
EPS_LN = 1.0e-5
EPS_Q = 1.0e-8
MAGIC = 12582912.0
TWO23 = 8388608.0

C = P // B
CW = S // C + 1
SK = T + C - 1
RW = CW + 1
LAST = S - 1 - (C - 1) * CW
PAD = C * CW

DIAG = 40.0
OUT = 128.0


def constants(np):
    p = np.arange(P)
    c = RW - np.arange(RW, dtype=np.float32)
    step = np.eye(P) + np.where((p[:, None] // C == p[None, :] // C) & (p[:, None] == p[None, :] + 1), 1 / OUT, 0)
    first = np.where(p % C == 0, 0, BIG)
    begin = np.where(p % C == C - 1, RW - 1 - LAST, 0)
    return {
        "identity": np.eye(P, dtype=np.float32),
        "walk_step": step.astype(np.float32),
        "codes": np.broadcast_to(np.concatenate([c, c + DIAG]), (P, 2 * RW)).astype(np.float32).copy(),
        "ends": np.stack([first, begin], 1).astype(np.float32),
    }


WB = 8
RECIP_BITS = float(0x7EF311C3)
I32 = mybir.dt.int32


def build(nc, x, ctx_in, w1, b1, w2, b2, identity, walk_step, codes_in, ends_in, out):
    with ExitStack() as stack:
        def sb(name, shape, dt=F32):
            return stack.enter_context(nc.sbuf_tensor(name, shape, dt))

        def sem(name):
            return stack.enter_context(nc.semaphore(name))

        big = sb("big", [P, 4 * NF * S])
        xq_store = sb("xq_store", [P, NF * S])
        w1q_store = sb("w1q_store", [P, 2 * Q * S])
        w2q_store = sb("w2q_store", [P, 2 * Q * S])
        ctx_rows = sb("ctx_rows", [P, B, D])
        ybuf = sb("ybuf", [P, 4, 512])
        ident = sb("ident", [P, P])
        identb = sb("identb", [P, P], BF16)
        walk = sb("walk", [P, P], BF16)
        codes = sb("codes", [P, 2 * RW])
        ends = sb("ends", [P, 2])
        stats = sb("stats", [P, 2, Q, 6])
        mv = sb("mv", [P, 2, Q, 2])
        small = sb("small", [P, 2, 7, Q])
        aa = sb("aa", [P, B])
        tiny = sb("tiny", [P, 1])
        magic = sb("magic", [P, 1])
        walked = sb("walked", [P, SK], BF16)
        wcodes = sb("wcodes", [P, 4, SK], BF16)
        span = sb("span", [P, 2, P])
        rmax = sb("rmax", [P, 2, Q])
        part = sb("part", [P, 8])
        ymax = sb("ymax", [P, NT + 4])
        wsc = sb("wsc", [P, 3, 20])
        bcol = sb("bcol", [P, NF + K])
        aff = sb("aff", [P, 6, NF])
        qrow = sb("qrow", [1, 8])
        qsc = sb("qsc", [P, 2, 2])
        onesr = sb("onesr", [1, P])
        hmax = sb("hmax", [P, B * 4 + 3])
        x2_dram = nc.dram_tensor("x2_dram", (B, P, Q, D), F32, kind="Internal").ap()
        h_dram = nc.dram_tensor("h_dram", (4, P, NF * S), F32, kind="Internal").ap()
        cost_dram = nc.dram_tensor("cost_dram", (B, C * (SK + 1) * CW), F32, kind="Internal").ap()
        s2_dram = nc.dram_tensor("s2_dram", (K, P), F32, kind="Internal").ap()
        b2_dram = nc.dram_tensor("b2_dram", (K, P), F32, kind="Internal").ap()

        half = 2 * NF * S
        X = big[:, 0:half].rearrange("p (b q d) -> p b q d", b=B, q=Q)
        Y2T = big[:, half:2 * half].rearrange("p (b k s) -> p b k s", b=B, k=K)
        H = big[:, :].rearrange("p (n f s) -> p n f s", n=4, f=NF)
        o = half
        R = big[:, o:o + (SK + 2) * RW]
        o += (SK + 2) * RW
        M = big[:, o:o + SK * RW]
        o += SK * RW
        COST = big[:, o:o + SK * CW]
        o += SK * CW
        L = big[:, o:o + SK * RW]
        o += SK * RW
        F = big[:, o:o + SK * RW]
        o += SK * RW
        assert o <= 2 * half
        ctxT = F[:, 0:K * B * T].rearrange("p (k n) -> p k n", k=K)
        dist = [z[:, 0:4 * PAD].rearrange("p (n s) -> p n s", n=4) for z in (R, M)]
        bbw = R[:, 4 * PAD:4 * PAD + 2 * Q * T].rearrange("p (n q i) -> p n q i", n=2, q=Q)
        tail = big[:, 2 * half - 2048:2 * half]
        spans = [tail[0:T, 264 * n:264 * n + 264].bitcast(BF16) for n in range(2)]
        path = [tail[0:T, 528 + 264 * n:792 + 264 * n].bitcast(BF16) for n in range(2)]
        HI, MID, LO = [xq_store[0:T, 2048 * n:2048 * n + 2048].bitcast(BF16).rearrange("p (b d) -> p b d", b=B)
                       for n in range(3)]
        RAW = xq_store[:, :].rearrange("p (n s) -> p n s", n=NF)
        XQ = xq_store[:, :].bitcast(BF16).rearrange("p (b k s) -> p b k s", b=B, k=K)
        HQ = xq_store[:, :].bitcast(BF16).rearrange("p (n f s) -> p n f s", n=2, f=NF)
        Y = w1q_store[:, :].rearrange("p (n q d) -> p n q d", n=2, q=Q)
        YT = w2q_store[:, :].rearrange("p (n k s) -> p n k s", n=2, k=K)
        W1 = w1q_store[:, :].bitcast(BF16).rearrange("p (k f) -> p k f", k=K)
        W2 = w2q_store[:, :].bitcast(BF16).rearrange("p (f d) -> p f d", f=NF)
        XB = w1q_store[:, :].rearrange("p (n q d) -> p n q d", n=2, q=Q)
        s2row = ctx_rows[:, 0, :]
        b2row = ctx_rows[:, 1, :]
        wqb = ybuf[:, :, :].rearrange("p n s -> p (n s)").bitcast(BF16).rearrange("p (n s) -> p n s", n=8)

        bank = [stack.enter_context(nc.psum_tensor(f"bank{n}", [P, 512], F32)) for n in range(8)]

        s_dve = sem("s_dve")
        s_way = sem("s_way")
        s_w2m = sem("s_w2m")
        s_small = sem("s_small")
        s_stat = sem("s_stat")
        s_aa = sem("s_aa")
        s_sq = sem("s_sq")
        s_e = sem("s_e")
        s_const = sem("s_const")
        s_ctx = sem("s_ctx")
        s_x = [sem(f"s_xin{b}") for b in range(B)]
        s_raw = [sem(f"s_raw{n}") for n in range(3)]
        s_zero = sem("s_zero")
        s_gz = sem("s_gz")
        s_gw = [sem(f"s_gw{n}") for n in range(2)]
        s_cost = sem("s_cost")
        s_tiny = sem("s_tiny")
        s_wmax = sem("s_wmax")
        s_ctp = sem("s_ctp")
        s_ctc = sem("s_ctc")
        s_var = sem("s_var")
        s_sd = sem("s_sd")
        s_y = sem("s_y")
        s_ytp = sem("s_ytp")
        s_ytc = sem("s_ytc")
        s_bb = sem("s_bb")
        s_d = sem("s_d")
        s_d2 = sem("s_d2")
        s_s0 = sem("s_s0")
        s_rc = sem("s_rc")
        s_c = sem("s_c")
        s_v = sem("s_v")
        s_wt = sem("s_wt")
        s_wq = sem("s_wq")
        s_wtp = sem("s_wtp")
        s_wtc = sem("s_wtc")
        s_dp = sem("s_dp")
        s_look = sem("s_look")
        s_step = sem("s_step")
        s_dsk = sem("s_dsk")
        s_dskp = sem("s_dskp")
        s_ab = sem("s_ab")
        s_path = sem("s_path")
        s_ex = sem("s_ex")
        s_hi = sem("s_hi")
        s_r1 = sem("s_r1")
        s_mid = sem("s_mid")
        s_lo = sem("s_lo")
        s_x2 = sem("s_x2")
        s_nb = sem("s_nb")
        s_y2 = sem("s_y2")
        s_y2p = sem("s_y2p")
        s_y2c = sem("s_y2c")
        s_spill = sem("s_spill")
        s_mx = sem("s_mx")
        s_mxp = sem("s_mxp")
        s_qr = sem("s_qr")
        s_qb = sem("s_qb")
        s_qs = sem("s_qs")
        s_xt = sem("s_xt")
        s_xg = sem("s_xg")
        s_xq = sem("s_xq")
        s_aff = sem("s_aff")
        s_l1 = sem("s_l1")
        s_h = sem("s_h")
        s_hm = sem("s_hm")
        s_hsp = [sem(f"s_hsp{n}") for n in range(4)]
        s_hre = [sem(f"s_hre{n}") for n in range(4)]
        s_ht = sem("s_ht")
        s_hq = sem("s_hq")
        s_xb = [sem(f"s_xb{n}") for n in range(2)]
        s_xbb = sem("s_xbb")
        s_l2 = sem("s_l2")
        s_o = sem("s_o")
        s_sum = sem("s_sum")
        s_out = [sem(f"s_out{n}") for n in range(2)]
        s_s2w = sem("s_s2w")
        s_s2r = sem("s_s2r")
        s_b1 = sem("s_b1")
        s_rows = sem("s_rows")
        s_b2w = sem("s_b2w")
        s_b2r = sem("s_b2r")

        block = stack.enter_context(nc.Block())

        x_v = x.rearrange("b (q p) d -> b p q d", p=P)
        out_v = out.rearrange("b (q p) d -> b p q d", p=P)
        w1_v = w1.rearrange("(n p) d -> p n d", p=P)
        w2_v = w2.rearrange("(n p) (h f) -> p n h f", p=P, h=4)
        order = [4, 5, 6, 7, 0, 1, 2, 3]

        @block.sync
        def _(sp):
            sp.dma_start(X[:, 0, :, :], x_v[0]).then_inc(s_x[0], 16)
            for dst, src in ((ident[:, :], identity), (ybuf[:, 0, 0:P], walk_step), (codes[:, :], codes_in),
                             (ends[:, :], ends_in)):
                sp.dma_start(dst, src).then_inc(s_const, 16)
            sp.dma_start(ctx_rows[0:T, :, :], ctx_in.rearrange("b i d -> i b d")).then_inc(s_ctx, 16)
            for b in range(1, 3):
                sp.dma_start(X[:, b, :, :], x_v[b]).then_inc(s_x[b], 16)
            for n in range(2):
                sp.dma_start(RAW[:, 8 * n:8 * n + 8, :], w1_v[:, 8 * n:8 * n + 8, :]).then_inc(s_raw[n], 16)
                sp.dma_start(X[:, 3 + n, :, :], x_v[3 + n]).then_inc(s_x[3 + n], 16)
            for b in range(5, B):
                sp.dma_start(X[:, b, :, :], x_v[b]).then_inc(s_x[b], 16)
            with nc.allow_non_contiguous_dma(reason="2048 words, off the critical path"):
                sp.dma_start(bcol[:, 0:NF], b1.rearrange("(n p) -> p n", p=P)).then_inc(s_b1, 16)
                sp.dma_start(bcol[:, NF:NF + K], b2.rearrange("(n p) -> p n", p=P)).then_inc(s_b1, 16)
            sp.wait_ge(s_zero, 1)
            for b in range(B):
                sp.dma_start(cost_dram[b, 0:C * SK * CW].rearrange("(c t) -> c t", c=C),
                             COST[C * b:C * b + C, :]).then_inc(s_gz, 16)
            sp.dma_start(cost_dram[:, C * SK * CW:].rearrange("b (o n) -> (b o) n", o=1),
                         COST[0:B, 0:C * CW]).then_inc(s_gz, 16)
            sp.wait_ge(s_gz, 16 * (B + 1))

            def read_costs(b):
                sp.wait_ge(s_gw[b % 2], 16 * (b // 2 + 1))
                sp.dma_start(COST[C * b:C * b + C, :],
                             cost_dram[b, 0:C * SK * CW].rearrange("(c t) -> c t", c=C)).then_inc(s_cost, 16)

            for b in range(B):
                sp.wait_ge(s_c, b + 1)
                skewed = cost_dram[b].rearrange("(c z) -> c z", c=C)[:, 0:T * CW]
                sp.dma_start(skewed.rearrange("c (i j) -> i c j", j=CW),
                             dist[b % 2][0:T, 3, :].rearrange("i (c j) -> i c j", j=CW)).then_inc(s_gw[b % 2], 16)
                if b >= 1:
                    read_costs(b - 1)
            read_costs(B - 1)
            sp.wait_ge(s_wq, NF)
            sp.dma_start(RAW.rearrange("p (n h) s -> p n h s", n=4), w2_v).then_inc(s_raw[2], 16)
            for b in range(B):
                sp.wait_ge(s_x2, (b + 1) * Q)
                sp.dma_start(x2_dram[b], X[:, b, :, :]).then_inc(s_spill, 16)
            sp.wait_ge(s_s2w, 16)
            sp.wait_ge(s_lo, B)
            sp.dma_start(s2row, s2_dram.rearrange("n (o p) -> o (n p)", o=1).broadcast_to([P, D])).then_inc(s_s2r, 16)
            for n in range(4):
                for g in range(4):
                    sp.wait_ge(s_h, n * NF + 4 * g + 4)
                    sp.dma_start(h_dram[n, :, g * 2048:g * 2048 + 2048],
                                 H[:, n, 4 * g:4 * g + 4, :]).then_inc(s_hsp[n], 16)
            for i in range(B):
                if i == 0:
                    sp.wait_ge(s_spill, 16 * B)
                    sp.wait_ge(s_l1, B * NF)
                if i >= 2:
                    sp.wait_ge(s_out[i % 2], 16 * (i // 2))
                sp.dma_start(XB[:, i % 2, :, :], x2_dram[order[i]]).then_inc(s_xb[i % 2], 16)
                if i == 0:
                    sp.wait_ge(s_rows, 1)
                    with nc.allow_non_contiguous_dma(reason="512 words"):
                        sp.dma_start(b2_dram.rearrange("n p -> p n"), aff[:, 1, 0:K]).then_inc(s_b2w, 16)
                    sp.wait_ge(s_b2w, 16)
                    sp.dma_start(b2row, b2_dram.rearrange("n (o p) -> o (n p)", o=1)
                                 .broadcast_to([P, D])).then_inc(s_b2r, 16)
                if i < 4:
                    for g in range(4):
                        sp.wait_ge(s_hq, 4 * i + g + 4)
                        if g == 0:
                            sp.wait_ge(s_hsp[i], 64)
                        sp.dma_start(H[:, i, 4 * g:4 * g + 4, :],
                                     h_dram[i, :, g * 2048:g * 2048 + 2048]).then_inc(s_hre[i], 16)
                if i >= 1:
                    sp.wait_ge(s_sum, Q * i)
                    sp.dma_start(out_v[order[i - 1]], XB[:, (i - 1) % 2, :, :]).then_inc(s_out[(i - 1) % 2], 16)
            for q in range(Q):
                sp.wait_ge(s_sum, Q * (B - 1) + q + 1)
                sp.dma_start(out_v[order[B - 1]][:, q, :], XB[:, (B - 1) % 2, q, :]).then_inc(s_out[(B - 1) % 2], 16)
            sp.wait_ge(s_out[0], 16 * B // 2)
            sp.wait_ge(s_out[1], 16 * (B // 2 - 1 + Q))

        @block.gpsimd
        def _(pool):
            g = nc.gpsimd
            g.memset(COST, 0.0).then_inc(s_zero, 1)
            g.memset(tiny[:, :], 1e-30).then_inc(s_tiny, 1)
            g.memset(onesr[:, :], 1.0).then_inc(s_tiny, 1)
            g.memset(magic[:, :], MAGIC).then_inc(s_tiny, 1)
            for n in range(2):
                g.memset(dist[n][0:T, 3, S:PAD], BIG).then_inc(s_tiny, 1)
            pool.wait_ge(s_const, 64)
            g.tensor_copy(identb[:, :], ident[:, :]).then_inc(s_tiny, 1)
            g.tensor_copy(walk[:, :], ybuf[:, 0, 0:P]).then_inc(s_tiny, 1)
            pool.wait_ge(s_tiny, 7)
            for b in range(B):
                t = dist[b % 2][0:T]
                pool.wait_ge(s_sq, b + 1)
                g.tensor_tensor(t[:, 2, 0:S], t[:, 0, 0:S], t[:, 2, 0:S], ALU.subtract).then_inc(s_v, 1)
                pool.wait_ge(s_v, b + 1)
                pool.wait_ge(s_rc, b + 1)
                g.tensor_tensor(t[:, 2, 0:S], t[:, 2, 0:S], t[:, 3, 0:S], ALU.mult).then_inc(s_e, 1)
            for n in range(2 * NF):
                pool.wait_ge(s_wt, n + 1)
                if n >= 8:
                    pool.wait_ge(s_wtp, n - 7)
                g.tensor_scalar(wqb[:, n % 8, :], RAW[:, n % NF, :], -MAGIC, 1.0, ALU.add,
                                ALU.mult).then_inc(s_wq, 1)
                if n in (NF + 3, NF + 7):
                    for b in range(n - NF - 3, n - NF + 1):
                        pool.wait_ge(s_hi, b + 1)
                        g.tensor_tensor(ctx_rows[0:T, b, :], ctx_rows[0:T, b, :], HI[:, b, :],
                                        ALU.subtract).then_inc(s_r1, 1)
                if n in (NF + 11, NF + 15):
                    pool.wait_ge(s_wq, NF + 12)
                    for b in range(n - NF - 11, n - NF - 7):
                        pool.wait_ge(s_mid, b + 1)
                        g.tensor_tensor(LO[:, b, :], ctx_rows[0:T, b, :], MID[:, b, :], ALU.subtract).then_inc(s_lo, 1)
            for b in range(B):
                pool.wait_ge(s_ab, b + 1)
                if b >= 2:
                    pool.wait_ge(s_ex, Q * (b - 1))
                g.tensor_tensor(path[b % 2], spans[0], spans[1], ALU.mult).then_inc(s_path, 1)
            pool.wait_ge(s_qs, 1)
            for b in range(1, B, 2):
                pool.wait_ge(s_y2c, (b + 1) * K)
                for k in range(K):
                    ins = g.tensor_scalar(Y2T[:, b, k, :], Y2T[:, b, k, :], qsc[:, 0, 1:2], MAGIC, ALU.mult, ALU.add)
                ins.then_inc(s_xg, 1)
            pool.wait_ge(s_b2r, 16)
            for i in range(B):
                pool.wait_ge(s_xb[i % 2], 16 * (i // 2 + 1))
                for q in range(Q):
                    g.tensor_tensor(XB[:, i % 2, q, :], XB[:, i % 2, q, :], b2row, ALU.add).then_inc(s_xbb, 1)
                for q in range(Q):
                    n = i * Q + q
                    pool.wait_ge(s_xbb, n + 1)
                    pool.wait_ge(s_o, n + 1)
                    g.tensor_tensor(XB[:, i % 2, q, :], XB[:, i % 2, q, :], ybuf[:, q, :], ALU.add).then_inc(s_sum, 1)

        @block.scalar
        def _(act):
            a = nc.scalar
            ID = ACT.Identity
            for n in range(2 * K):
                act.wait_ge(s_ctp, n + 1)
                k, h = n // 2, n % 2
                a.activation(ctxT[:, k, 4 * T * h:4 * T * h + 4 * T], bank[n % 4][:, 0:4 * T], ID).then_inc(s_ctc, 1)

            def root(n, wait):
                act.wait_ge(s_var, wait)
                a.activation(small[:, n % 2, 1, :], small[:, n % 2, 0, :], ACT.Sqrt).then_inc(s_sd, 1)

            def costs(b):
                t = dist[b % 2][0:T]
                act.wait_ge(s_d, b + 1)
                if b >= 2:
                    act.wait_ge(s_c, b - 1)
                a.activation(t[:, 0, 0:S], bank[4 + b % 2][0:T, :], ACT.Relu, bias=aa[0:T, b:b + 1],
                             scale=-2.0).then_inc(s_d2, 1)
                act.wait_ge(s_d2, b + 1)
                a.activation(t[:, 1, 0:S], t[:, 0, 0:S], ACT.Sqrt, bias=tiny[0:T, :]).then_inc(s_s0, 1)
                act.wait_ge(s_s0, b + 1)
                a.activation(t[:, 2, 0:S], t[:, 1, 0:S], ACT.Square).then_inc(s_sq, 1)

            act.wait_ge(s_tiny, 7)
            root(0, 1)
            for b in range(B):
                if b >= 2:
                    act.wait_ge(s_aa, b - 1)
                a.activation(ybuf[0:T, 1 + b % 2, :], ctx_rows[0:T, b, :], ACT.Square,
                             accum_out=aa[0:T, b:b + 1]).then_inc(s_aa, 1)
            act.wait_ge(s_aa, B)
            root(1, 2)
            for b in range(B):
                if b >= 2:
                    act.wait_ge(s_d, b - 1)
                for k in range(K):
                    act.wait_ge(s_ytp, b * K + k + 1)
                    a.activation(YT[:, b % 2, k, :], bank[k][:, :], ID).then_inc(s_ytc, 1)
                if b >= 1:
                    costs(b - 1)
                if b + 2 < B:
                    root(b, b + 3)
            costs(B - 1)

            def weights(n):
                if n >= NF and n % 4 == 0:
                    act.wait_ge(s_wmax, 2 + (n - NF) // 4)
                col = n if n < NF else NF + (n - NF) // 4
                a.activation(RAW[:, n % NF, :], RAW[:, n % NF, :], ID, bias=magic[:, :],
                             scale=wsc[:, 2, col:col + 1]).then_inc(s_wt, 1)

            def turned(m):
                act.wait_ge(s_wtp, m + 1)
                src = bank[m % 4][:, 0:256].bitcast(BF16).rearrange("p (k f) -> p k f", k=4)
                if m < NF:
                    dst = W1[:, :, m * P:m * P + P]
                else:
                    dt_, h = (m - NF) // 4, (m - NF) % 4
                    dst = W2[:, 4 * h:4 * h + 4, dt_ * P:dt_ * P + P]
                a.activation(dst, src, ID).then_inc(s_wtc, 1)

            act.wait_ge(s_wmax, 1)
            for n in range(NF + 2):
                if n < NF:
                    weights(n)
                if n >= 2:
                    turned(n - 2)
            for t in range(5):
                if t < 4:
                    for n in range(NF + 4 * t, NF + 4 * t + 4):
                        weights(n)
                if t == 0:
                    act.wait_ge(s_wq, NF + 4)
                    for b in range(B):
                        a.activation(HI[:, b, :], ctx_rows[0:T, b, :], ID).then_inc(s_hi, 1)
                else:
                    for n in range(NF + 4 * t - 4, NF + 4 * t):
                        turned(n)
                if t == 1:
                    act.wait_ge(s_wq, NF + 8)
                    for b in range(B):
                        act.wait_ge(s_r1, b + 1)
                        a.activation(MID[:, b, :], ctx_rows[0:T, b, :], ID).then_inc(s_mid, 1)

            with nc.allow_non_contiguous_dma(reason="512 words, off the critical path"):
                act.dma_start(s2_dram.rearrange("n p -> p n"), wsc[:, 1, NF:NF + 4]).then_inc(s_s2w, 16)

            def tokens_up(b):
                a.activation(Y2T[:, b, :, :], Y2T[:, b, :, :], ID, bias=magic[:, :],
                             scale=qsc[:, 0, 1:2]).then_inc(s_xt, 1)

            root(0, B + 1)
            for b in range(B):
                act.wait_ge(s_nb, b + 1)
                if b >= 1:
                    act.wait_ge(s_y2p, K * b)
                for q in range(Q):
                    a.activation(ybuf[:, q, :], X[:, b, q, :], ID, bias=small[:, b % 2, 6, q:q + 1],
                                 scale=small[:, b % 2, 5, q:q + 1]).then_inc(s_y2, 1)
                if b + 1 < B:
                    root(b + 1, B + b + 2)
                else:
                    act.wait_ge(s_qs, 1)
                    tokens_up(0)
                for k in range(K):
                    act.wait_ge(s_y2p, b * K + k + 1)
                    a.activation(Y2T[:, b, k, :], bank[k][:, :], ID).then_inc(s_y2c, 1)

            act.wait_ge(s_y2c, B * K)
            tokens_up(2)
            act.wait_ge(s_aff, 1)
            act.wait_ge(s_spill, 16 * B)
            for n in range(B):
                if n == 2:
                    act.wait_ge(s_xq, B)
                for f in range(NF):
                    if n >= 4 and f == 0:
                        act.wait_ge(s_hsp[n - 4], 64)
                    act.wait_ge(s_l1, n * NF + f + 1)
                    if n >= 4 and f % 4 == 0:
                        act.wait_ge(s_hm, (n - 4) * 4 + f // 4 + 1)
                    a.activation(H[:, n % 4, f, :], bank[f % 8][:, :], ACT.Relu, bias=aff[:, 1, f:f + 1],
                                 scale=aff[:, 0, f:f + 1]).then_inc(s_h, 1)
                    if n * NF + f in (7, 15):
                        tokens_up(4 + 2 * (f // 8))
            act.wait_ge(s_qs, 2)
            for i in range(B):
                for g in range(4):
                    if i >= 4:
                        act.wait_ge(s_hre[i - 4], 64)
                    for f, m in [(f, 1) for f in range(4)] if i + g == 0 else [(4 * g, 4)]:
                        a.activation(H[:, i % 4, f:f + m, :], H[:, i % 4, f:f + m, :], ID,
                                     bias=magic[:, :], scale=qsc[:, 1, 1:2]).then_inc(s_ht, 1)

        @block.vector
        def _(dve):
            v = nc.vector
            chain = [0]

            def link(ins):
                chain[0] += 1
                ins.then_inc(s_dve, 1)
                dve.wait_ge(s_dve, chain[0])

            smalls = [0]

            def small_done(ins):
                smalls[0] += 1
                ins.then_inc(s_small, 1)

            def after_small():
                dve.wait_ge(s_small, smalls[0])

            def one_bn(b, q, src, base):
                v.bn_stats(stats[:, b % 2, q, :], src).then_inc(s_stat, 1)

            def rsqrt_step(b, n):
                m = small[:, b % 2]
                after_small()
                if n == 0:
                    small_done(v.reciprocal(m[:, 2, :], m[:, 1, :]))
                elif n == 1:
                    small_done(v.tensor_tensor(m[:, 3, :], m[:, 2, :], m[:, 2, :], ALU.mult))
                elif n == 2:
                    small_done(v.tensor_tensor(m[:, 3, :], m[:, 3, :], m[:, 0, :], ALU.mult))
                elif n == 3:
                    small_done(v.tensor_scalar(m[:, 3, :], m[:, 3, :], -0.5, 1.5, ALU.mult, ALU.add))
                else:
                    small_done(v.tensor_tensor(m[:, 5, :], m[:, 2, :], m[:, 3, :], ALU.mult))

            def variance(b, n):
                dve.wait_ge(s_stat, n)
                for q in range(Q):
                    v.bn_aggr(mv[:, b % 2, q, :], stats[:, b % 2, q, :]).then_inc(s_small, 1)
                smalls[0] += Q
                after_small()
                v.tensor_scalar(small[:, b % 2, 0, :], mv[:, b % 2, :, 1], EPS_LN, None, ALU.add).then_inc(s_var, 1)

            def w1_max(n):
                if n % 8 == 0:
                    dve.wait_ge(s_raw[n // 8], 16)
                v.tensor_reduce(wsc[:, 0, n:n + 1], RAW[:, n, :], AX, ALU.max,
                                apply_absolute_value=True).then_inc(s_dve, 1)
                chain[0] += 1

            for b in range(B + 4):
                p = b - 1
                if b < B:
                    dve.wait_ge(s_x[b], 16)
                for q in range(Q):
                    if b < B:
                        v.bn_stats(stats[:, b % 2, q, :], X[:, b, q, :]).then_inc(s_stat, 1)
                    if 0 <= p < B:
                        if q == 0:
                            dve.wait_ge(s_sd, p + 1)
                        rsqrt_step(p, q)
                if 0 <= p < B:
                    rsqrt_step(p, 4)
                    m = small[:, p % 2]
                    after_small()
                    small_done(v.tensor_tensor(m[:, 4, :], m[:, 5, :], m[:, 5, :], ALU.mult))
                if b < B:
                    variance(b, Q * (b + 1))
                if 0 <= p < B:
                    if p >= 2:
                        dve.wait_ge(s_ytp, K * (p - 1))
                    for q in range(Q):
                        v.tensor_scalar(Y[:, p % 2, q, :], X[:, p, q, :], mv[:, p % 2, q, 0:1], m[:, 5, q:q + 1],
                                        ALU.subtract, ALU.mult).then_inc(s_y, 1)
                    after_small()
                    small_done(v.tensor_tensor(m[:, 4, :], m[:, 4, :], mv[:, p % 2, :, 1], ALU.mult))
                if b - 3 >= 0 and b - 3 < B:
                    n = b - 3
                    t = dist[n % 2][0:T]
                    dve.wait_ge(s_s0, n + 1)
                    if n >= 2:
                        dve.wait_ge(s_gw[n % 2], 16 * (n // 2))
                    v.tensor_scalar(t[:, 3, 0:S].bitcast(I32), t[:, 1, 0:S].bitcast(I32), -1.0, RECIP_BITS, ALU.mult,
                                    ALU.add).then_inc(s_rc, 1)
                if 3 <= b < 11:
                    w1_max(2 * (b - 3))
                if 0 <= p < B:
                    after_small()
                    if p >= 2:
                        dve.wait_ge(s_d, p - 1)
                    v.tensor_scalar(bbw[:, p % 2, :, :], m[:, 4, :].unsqueeze(2).broadcast_to([P, Q, T]), -0.5 * D,
                                    None, ALU.mult).then_inc(s_bb, 1)
                if 3 <= b < 11:
                    w1_max(2 * (b - 3) + 1)
                if b - 3 >= 0 and b - 3 < B:
                    dve.wait_ge(s_e, n + 1)
                    v.scalar_tensor_tensor(out=t[:, 3, 0:S], in0=t[:, 1, 0:S], scalar=2.0, in1=t[:, 2, 0:S],
                                           op0=ALU.mult, op1=ALU.add).then_inc(s_c, 1)
            dve.wait_ge(s_dve, chain[0])
            link(v.tensor_scalar(wsc[:, 1, 0:NF], wsc[:, 0, 0:NF], EPS_Q, 1.0 / 127.0, ALU.max, ALU.mult))
            v.reciprocal(wsc[:, 2, 0:NF], wsc[:, 1, 0:NF]).then_inc(s_wmax, 1)

            def row(t, a, n):
                return R[:, t * RW + a:t * RW + a + n]

            left = [C * (i // C) + (i % C - 1) % C for i in range(32)]
            for n in range(2):
                dve.wait_ge(s_gw[n], 16 * B // 2)
            link(v.memset(R[:, 0:2 * RW], BIG))
            link(v.tensor_copy(R[:, 0:1], ends[:, 0:1]))
            R3 = R.rearrange("p (t j) -> p t j", j=RW)
            L3 = L.rearrange("p (t j) -> p t j", j=RW)
            F3 = F.rearrange("p (t j) -> p t j", j=RW)
            v.memset(L3[:, :, 0:1], 0.0).then_inc(s_dve, 1)
            v.memset(F3[:, :, 0:1], OUT).then_inc(s_dve, 1)
            chain[0] += 2
            v.tensor_tensor(M[:, 0:CW], row(0, 1, CW), row(0, 0, CW), ALU.min).then_inc(s_dp, 1)
            dve.wait_ge(s_cost, 16 * B)
            for t in range(SK):
                dve.wait_ge(s_dp, 1 + 3 * t)
                v.tensor_tensor_scan(row(t + 1, 1, CW), M[:, t * CW:t * CW + CW], COST[:, t * CW:t * CW + CW],
                                     row(t + 1, 0, 1), ALU.min, ALU.add).then_inc(s_dp, 1)
                v.tensor_tensor(F3[:, t, 1:RW], row(t, 0, CW), row(t, 1, CW), ALU.is_le).then_inc(s_dve, 1)
                dve.wait_ge(s_dp, 2 + 3 * t)
                if t + 1 < SK:
                    v.tensor_tensor(M[:, (t + 1) * CW:(t + 2) * CW], row(t + 1, 1, CW), row(t + 1, 0, CW),
                                    ALU.min).then_inc(s_dp, 1)
                    v.stream_shuffle(row(t + 2, 0, 1), row(t + 1, CW, 1), left).then_inc(s_dp, 1)
                v.tensor_tensor(L3[:, t, 1:RW], row(t + 1, 0, CW), M[:, t * CW:t * CW + CW],
                                ALU.is_lt).then_inc(s_dve, 1)
            chain[0] += 2 * SK
            dve.wait_ge(s_dve, chain[0])

            N3 = M.rearrange("p (t j) -> p t j", j=RW)

            def way_on(k, n):
                e = SK - k * WB
                a = max(e - WB, 0)
                if e <= 0:
                    return
                if n == 0:
                    v.scalar_tensor_tensor(out=F3[:, a:e, 1:RW], in0=F3[:, a:e, 1:RW], scalar=DIAG + 1,
                                           in1=codes[:, 1:RW].unsqueeze(1).broadcast_to([P, e - a, CW]),
                                           op0=ALU.mult, op1=ALU.add).then_inc(s_way, 1)
                elif n == 1:
                    dve.wait_ge(s_way, 3 * k + 1)
                    v.scalar_tensor_tensor(out=F3[:, a:e, 1:RW], in0=L3[:, a:e, 1:RW], scalar=0.0,
                                           in1=F3[:, a:e, 1:RW], op0=ALU.is_equal, op1=ALU.mult).then_inc(s_way, 1)
                else:
                    dve.wait_ge(s_way, 3 * k + 2)
                    v.tensor_tensor_scan(M[:, a * RW:e * RW], L[:, a * RW:e * RW], F[:, a * RW:e * RW], OUT,
                                         ALU.mult, ALU.add).then_inc(s_way, 1)

            def w2_max(j):
                n, i = j // 11, j % 11
                if n >= K:
                    return
                col = wsc[:, :, NF + n:NF + n + 1]
                if j == 0:
                    dve.wait_ge(s_raw[2], 16)
                if i < 8:
                    if i == 0 and n:
                        dve.wait_ge(s_w2m, 10 * n)
                    v.tensor_reduce(part[:, i:i + 1], RAW[:, 4 * n + i // 2, 256 * (i % 2):256 * (i % 2) + 256], AX,
                                    ALU.max, apply_absolute_value=True).then_inc(s_w2m, 1)
                elif i == 8:
                    dve.wait_ge(s_w2m, 10 * n + 8)
                    v.tensor_reduce(col[:, 0, :], part[:, :], AX, ALU.max).then_inc(s_w2m, 1)
                elif i == 9:
                    dve.wait_ge(s_w2m, 10 * n + 9)
                    v.tensor_scalar(col[:, 1, :], col[:, 0, :], EPS_Q, 1.0 / 127.0, ALU.max,
                                    ALU.mult).then_inc(s_w2m, 1)
                else:
                    dve.wait_ge(s_w2m, 10 * n + 10)
                    v.reciprocal(col[:, 2, :], col[:, 1, :]).then_inc(s_wmax, 1)

            for n in range(3):
                way_on(0, n)

            both = codes[:, :].rearrange("p (n j) -> p n j", n=2)
            junk = COST[:, 0:2 * RW].rearrange("p (n j) -> p n j", n=2)
            for n in range(SK):
                t = SK - 1 - n
                if n:
                    dve.wait_ge(s_step, n)
                if n % WB == 0:
                    dve.wait_ge(s_way, 3 * (n // WB) + 3)
                at = ends[:, 1:2] if n == 0 else bank[6][:, t:t + 1]
                v.scalar_tensor_tensor(out=junk, in0=both, scalar=at,
                                       in1=N3[:, t, :].unsqueeze(1).broadcast_to([P, 2, RW]), op0=ALU.is_equal,
                                       op1=ALU.mult, accum_out=walked[:, t:t + 1]).then_inc(s_look, 1)
                if n % WB < 3:
                    way_on(n // WB + 1, n % WB)
                else:
                    w2_max((WB - 3) * (n // WB) + n % WB - 3)
            dve.wait_ge(s_look, SK)
            link(v.tensor_copy(wcodes[:, 0, SK - 1:SK], ends[:, 1:2]))
            link(v.tensor_copy(wcodes[:, 0, 0:SK - 1], bank[6][:, 0:SK - 1]))
            link(v.tensor_scalar(wcodes[:, 1, :], wcodes[:, 0, :], DIAG + 0.5, -DIAG, ALU.is_ge, ALU.mult))
            link(v.tensor_tensor(wcodes[:, 2, :], wcodes[:, 0, :], wcodes[:, 1, :], ALU.add))
            link(v.tensor_scalar(wcodes[:, 1, :], walked[:, :], DIAG + 0.5, -DIAG - 1, ALU.is_ge, ALU.mult))
            v.tensor_tensor(wcodes[:, 3, :], walked[:, :], wcodes[:, 1, :], ALU.add).then_inc(s_dsk, 1)
            dve.wait_ge(s_dskp, 1)
            link(v.tensor_copy(span[0:T, :, :], bank[7][0:T, 0:2 * P].rearrange("p (n c) -> p n c", n=2)))

            def on_path(b):
                c3 = codes[0:T, 1:RW].unsqueeze(1).broadcast_to([T, C, CW])
                sp3 = span[0:T, :, :].rearrange("p n (c b) -> p n b c", b=B)
                if b >= 1:
                    dve.wait_ge(s_path, b)
                for n, op in ((0, ALU.is_ge), (1, ALU.is_le)):
                    ins = v.tensor_tensor(spans[n].rearrange("p (c j) -> p c j", c=C), c3,
                                          sp3[:, n, b, :].unsqueeze(2).broadcast_to([T, C, CW]), op)
                ins.then_inc(s_ab, 1)

            on_path(0)
            on_path(1)
            for b in range(B + 1):
                p = b - 1
                m = small[:, p % 2]
                if b >= 2:
                    dve.wait_ge(s_y2, Q * (b - 1))
                for q in range(Q):
                    n = b * Q + q
                    if b < B:
                        dve.wait_ge(s_ex, n + 1)
                        v.tensor_tensor_reduce(X[:, b, q, :], bank[4 + n % 4][:, :], X[:, b, q, :], 1.0, -3.0e38,
                                               ALU.add, ALU.max, rmax[:, b % 2, q:q + 1]).then_inc(s_x2, 1)
                    if p >= 0:
                        if q == 0:
                            dve.wait_ge(s_sd, B + p + 1)
                        rsqrt_step(p, q)
                for q in range(Q):
                    if b < B:
                        dve.wait_ge(s_x2, b * Q + q + 1)
                        v.bn_stats(stats[:, b % 2, q, :], X[:, b, q, :]).then_inc(s_stat, 1)
                    if p >= 0 and q == 0:
                        rsqrt_step(p, 4)
                    elif p >= 0 and q == 1:
                        after_small()
                        v.scalar_tensor_tensor(out=m[:, 6, :], in0=mv[:, p % 2, :, 0], scalar=-1.0, in1=m[:, 5, :],
                                               op0=ALU.mult, op1=ALU.mult).then_inc(s_nb, 1)
                        small_done(v.tensor_tensor(m[:, 4, :], rmax[:, p % 2, :], mv[:, p % 2, :, 0], ALU.subtract))
                    elif p >= 0 and q == 2:
                        after_small()
                        small_done(v.tensor_tensor(ymax[:, p * Q:p * Q + Q], m[:, 4, :], m[:, 5, :], ALU.mult))
                if b < B:
                    variance(b, Q * (B + b + 1))
                if b + 2 < B:
                    on_path(b + 2)
            after_small()

            def step_size(n, src):
                v.tensor_reduce(ymax[:, NT + n:NT + n + 1], src, AX, ALU.max).then_inc(s_mx, 1)
                dve.wait_ge(s_mxp, n + 1)
                link(v.tensor_reduce(qrow[:, 0:1], bank[7][0:1, 0:P], AX, ALU.max))
                link(v.tensor_scalar(qrow[:, 1:2], qrow[:, 0:1], EPS_Q, 1.0 / 255.0, ALU.max, ALU.mult))
                v.reciprocal(qrow[:, 2:3], qrow[:, 1:2]).then_inc(s_qr, 1)
                dve.wait_ge(s_qb, n + 1)
                v.tensor_copy(qsc[:, n, :], bank[6][:, 0:2]).then_inc(s_qs, 1)
                dve.wait_ge(s_qs, n + 1)

            def on_grid(dst, bias, scale, t, done):
                link(v.reciprocal(t[0], scale))
                link(v.tensor_tensor(t[0], bias, t[0], ALU.mult))
                link(v.scalar_tensor_tensor(out=t[1], in0=t[0], scalar=-1.0, in1=t[0], op0=ALU.mult, op1=ALU.max))
                link(v.tensor_scalar(t[2], t[1], TWO23, TWO23, ALU.add, ALU.subtract))
                link(v.tensor_tensor(t[3], t[1], t[2], ALU.subtract))
                link(v.scalar_tensor_tensor(out=t[3], in0=t[1], scalar=TWO23, in1=t[3], op0=ALU.is_ge, op1=ALU.mult))
                link(v.tensor_tensor(t[2], t[2], t[3], ALU.add))
                link(v.tensor_scalar(t[0], t[0], 0.0, 2.0, ALU.is_ge, ALU.mult))
                link(v.scalar_tensor_tensor(out=t[2], in0=t[0], scalar=-1.0, in1=t[2], op0=ALU.add, op1=ALU.mult))
                v.tensor_tensor(dst, t[2], scale, ALU.mult).then_inc(done, 1)

            step_size(0, ymax[:, 0:NT])

            def tokens_down(b):
                dve.wait_ge(s_xg if b % 2 else s_xt, b // 2 + 1)
                v.tensor_scalar(XQ[:, b, :, :], Y2T[:, b, :, :], MAGIC, 0.0, ALU.subtract, ALU.max).then_inc(s_xq, 1)

            dve.wait_ge(s_wtp, 2 * NF)
            tokens_down(0)
            link(v.tensor_scalar(aff[:, 0, :], wsc[:, 1, 0:NF], qsc[:, 0, 0:1], None, ALU.mult))
            dve.wait_ge(s_b1, 32)
            on_grid(aff[:, 1, :], bcol[:, 0:NF], aff[:, 0, :], [aff[:, 2 + i, :] for i in range(4)], s_aff)
            for b in range(1, B):
                tokens_down(b)
            for n in range(B * 4 - 1):
                dve.wait_ge(s_h, 4 * n + 4)
                tb, g = n // 4, n % 4
                v.tensor_reduce(hmax[:, n:n + 1], H[:, tb % 4, 4 * g:4 * g + 4, :].rearrange("p f s -> p (f s)"), AX,
                                ALU.max).then_inc(s_hm, 1)
            for f in range(NF - 4, NF):
                dve.wait_ge(s_h, (B - 1) * NF + f + 1)
                n = B * 4 - 1 + f - (NF - 4)
                v.tensor_reduce(hmax[:, n:n + 1], H[:, (B - 1) % 4, f, :], AX, ALU.max).then_inc(s_hm, 1)
            dve.wait_ge(s_hm, B * 4 + 3)
            step_size(1, hmax[:, :])
            link(v.tensor_scalar(aff[:, 0, 0:K], wsc[:, 1, NF:NF + K], qsc[:, 1, 0:1], None, ALU.mult))
            on_grid(aff[:, 1, 0:K], bcol[:, NF:NF + K], aff[:, 0, 0:K], [aff[:, 2 + i, 0:K] for i in range(4)], s_rows)
            dve.wait_ge(s_s2r, 16)

            def hidden(i):
                for g in range(4):
                    if i >= 2 and g == 0:
                        dve.wait_ge(s_l2, Q * (i - 1))
                    for f, m in [(f, 1) for f in range(4)] if i + g == 0 else [(4 * g, 4)]:
                        dve.wait_ge(s_ht, f + 1 if m == 1 else 4 * i + g + 4)
                        v.tensor_scalar(HQ[:, i % 2, f:f + m, :], H[:, i % 4, f:f + m, :], MAGIC, 255.0,
                                        ALU.subtract, ALU.min).then_inc(s_hq, 1)

            hidden(0)
            link(v.tensor_scalar(s2row, s2row, qsc[:, 1, 0:1], None, ALU.mult))
            for i in range(B):
                if i + 1 < B:
                    hidden(i + 1)
                for q in range(Q):
                    n = i * Q + q
                    dve.wait_ge(s_l2, n + 1)
                    if n >= 4:
                        dve.wait_ge(s_sum, n - 3)
                    v.tensor_tensor(ybuf[:, q, :], bank[n % 4][:, :], s2row, ALU.mult).then_inc(s_o, 1)

        @block.tensor
        def _(pe):
            t = nc.tensor
            pe.wait_ge(s_ctx, 16)
            pe.wait_ge(s_const, 64)
            for n in range(2 * K):
                k, h = n // 2, n % 2
                if n >= 4:
                    pe.wait_ge(s_ctc, n - 3)
                for j in range(4):
                    last = t.transpose(bank[n % 4][:, T * j:T * j + T],
                                       ctx_rows[0:T, 4 * h + j, k * P:k * P + P], ident[0:T, 0:T])
                last.then_inc(s_ctp, 1)

            def turn(b):
                for k in range(K):
                    if b == 0 and k == 0:
                        pe.wait_ge(s_ctc, 2 * K)
                    if b >= 1:
                        pe.wait_ge(s_ytc, (b - 1) * K + k + 1)
                    for q in range(Q):
                        if k == 0:
                            pe.wait_ge(s_y, b * Q + q + 1)
                        last = t.transpose(bank[k][:, q * P:q * P + P], Y[:, b % 2, q, k * P:k * P + P], ident[:, :])
                    last.then_inc(s_ytp, 1)

            def distances(b):
                d = bank[4 + b % 2][0:T, :]
                pe.wait_ge(s_ytc, (b + 1) * K)
                if b >= 2:
                    pe.wait_ge(s_d2, b - 1)
                pe.wait_ge(s_bb, b + 1)
                for k in range(K):
                    t.matmul(d, ctxT[:, k, b * T:b * T + T], YT[:, b % 2, k, :], start=(k == 0), stop=False)
                for q in range(Q):
                    last = t.matmul(d[:, q * P:q * P + P], bbw[:, b % 2, q, :], ident[:, :], start=False,
                                    stop=(q == Q - 1))
                last.then_inc(s_d, 1)

            for b in range(B):
                turn(b)
                if b >= 1:
                    distances(b - 1)
            distances(B - 1)

            def turn_weights(n, k):
                if k == 0:
                    pe.wait_ge(s_wq, n + 1)
                    if n == 0:
                        pe.wait_ge(s_ytc, B * K)
                    if n >= 4:
                        pe.wait_ge(s_wtc, n - 3)
                ins = t.transpose(bank[n % 4][:, 64 * k:64 * k + 64].bitcast(BF16), wqb[:, n % 8, k * P:k * P + P],
                                  identb[:, :])
                if k == 3:
                    ins.then_inc(s_wtp, 1)

            for n in range(NF):
                for k in range(4):
                    turn_weights(n, k)

            for n in range(SK - 1):
                c = SK - 1 - n
                pe.wait_ge(s_look, n + 1)
                t.matmul(bank[6][:, c - 1:c], walk[:, :], walked[:, c:c + 1], start=True, stop=True).then_inc(s_step, 1)
                if n >= 31:
                    turn_weights(NF + (n - 31) // 4, (n - 31) % 4)
            for j in range(SK - 1 - 31, 4 * NF):
                turn_weights(NF + j // 4, j % 4)

            pe.wait_ge(s_dsk, 1)
            for n in range(2):
                for c in range(C):
                    last = t.matmul(bank[7][0:T, n * P + c * B:n * P + c * B + B], wcodes[:, 2 + n, c:c + T],
                                    identb[:, c:c + C * (B - 1) + 1:C], start=True, stop=True)
            last.then_inc(s_dskp, 1)

            def gather(b):
                pe.wait_ge(s_path, b + 1)
                pe.wait_ge(s_lo, b + 1)
                for q in range(Q):
                    n = b * Q + q
                    if n == 0:
                        pe.wait_ge(s_d2, B)
                    if n >= 4:
                        pe.wait_ge(s_x2, n - 3)
                    for part_, first in ((HI, True), (MID, False), (LO, False)):
                        last = t.matmul(bank[4 + n % 4][:, :], path[b % 2][:, q * P:q * P + P], part_[:, b, :],
                                        start=first, stop=(part_ is LO))
                    last.then_inc(s_ex, 1)

            def turn2(b):
                for k in range(K):
                    if b == 0 and k == 0:
                        pe.wait_ge(s_wtc, 2 * NF)
                    if b >= 1:
                        pe.wait_ge(s_y2c, (b - 1) * K + k + 1)
                    for q in range(Q):
                        if k == 0:
                            pe.wait_ge(s_y2, b * Q + q + 1)
                        last = t.transpose(bank[k][:, q * P:q * P + P], ybuf[:, q, k * P:k * P + P], ident[:, :])
                    last.then_inc(s_y2p, 1)

            def spread(n):
                pe.wait_ge(s_mx, n + 1)
                t.transpose(bank[7][0:1, 0:P], ymax[:, NT + n:NT + n + 1], ident[:, :]).then_inc(s_mxp, 1)
                pe.wait_ge(s_qr, n + 1)
                t.matmul(bank[6][:, 0:2], onesr[:, :], qrow[:, 1:3], start=True, stop=True).then_inc(s_qb, 1)

            gather(0)
            gather(1)
            for b in range(B):
                if b + 2 < B:
                    gather(b + 2)
                elif b == B - 1:
                    pe.wait_ge(s_x2, B * Q)
                    spread(0)
                turn2(b)
            pe.wait_ge(s_qs, 1)
            pe.wait_ge(s_y2c, B * K)
            for b in range(B):
                pe.wait_ge(s_xq, b + 1)
                for f in range(NF):
                    n = b * NF + f
                    if n >= 8:
                        pe.wait_ge(s_h, n - 7)
                    for k in range(K):
                        last = t.matmul(bank[f % 8][:, :], W1[:, k, f * P:f * P + P], XQ[:, b, k, :],
                                        start=(k == 0), stop=(k == K - 1))
                    last.then_inc(s_l1, 1)
            pe.wait_ge(s_h, B * NF)
            spread(1)
            for g in range(4):
                for q in range(Q):
                    for f in range(4 * g, 4 * g + 4):
                        if q == 0:
                            pe.wait_ge(s_hq, f + 1 if g == 0 else g + 4)
                        last = t.matmul(bank[q][:, :], HQ[:, 0, f, q * P:q * P + P], W2[:, f, :],
                                        start=(f == 0), stop=(f == NF - 1))
                    if g == 3:
                        last.then_inc(s_l2, 1)
            for i in range(1, B):
                for q in range(Q):
                    n = i * Q + q
                    pe.wait_ge(s_o, n - 3)
                    for f in range(NF):
                        if q == 0 and f % 4 == 0:
                            pe.wait_ge(s_hq, 4 * i + f // 4 + 4)
                        last = t.matmul(bank[n % 4][:, :], HQ[:, i % 2, f, q * P:q * P + P], W2[:, f, :],
                                        start=(f == 0), stop=(f == NF - 1))
                    last.then_inc(s_l2, 1)


_INS = ["x", "ctx_1024", "L0_ffn_w1", "L0_ffn_b1", "L0_ffn_w2", "L0_ffn_b2"]


def kernel(**inputs):
    import numpy as np
    import concourse.bacc as bacc
    from concourse.bass_utils import run_bass_kernel_spmd as run

    nc = bacc.Bacc("TRN2", target_bir_lowering=False, num_devices=1, dynamic_dma_scratch_size=1024)
    arrays, args = {}, []
    for name in _INS:
        arrays[f"in_{name}"] = np.ascontiguousarray(inputs[name])
    for name, a in constants(np).items():
        arrays[f"const_{name}"] = a
    for name, a in arrays.items():
        args.append(nc.dram_tensor(name, a.shape, mybir.dt.from_np(a.dtype), kind="ExternalInput").ap())
    out = nc.dram_tensor("out_0", (B, S, D), F32, kind="ExternalOutput").ap()
    build(nc, *args, out)
    r = run(nc, [arrays], core_ids=[0])
    return r.results[0]["out_0"]
```

```python
import concourse.bass as bass
from concourse import mybir
from concourse.alu_op_type import AluOpType as ALU
from contextlib import ExitStack

ACT = mybir.ActivationFunctionType
AX = mybir.AxisListType.X
F32 = mybir.dt.float32
BF16 = mybir.dt.bfloat16

P = 128
B, S, D = 8, 512, 512
T = 77
FF = 2048
Q = S // P
K = D // P
NF = FF // P
NT = B * Q
BIG = 1.0e30
EPS_LN = 1.0e-5
EPS_Q = 1.0e-8
MAGIC = 12582912.0
TWO23 = 8388608.0

C = P // B
CW = S // C + 1
SK = T + C - 1
RW = CW + 1
LAST = S - 1 - (C - 1) * CW
PAD = C * CW

DIAG = 40.0
OUT = 128.0


def constants(np):
    p = np.arange(P)
    c = RW - np.arange(RW, dtype=np.float32)
    step = np.eye(P) + np.where((p[:, None] // C == p[None, :] // C) & (p[:, None] == p[None, :] + 1), 1 / OUT, 0)
    first = np.where(p % C == 0, 0, BIG)
    begin = np.where(p % C == C - 1, RW - 1 - LAST, 0)
    return {
        "identity": np.eye(P, dtype=np.float32),
        "walk_step": step.astype(np.float32),
        "codes": np.broadcast_to(np.concatenate([c, c + DIAG]), (P, 2 * RW)).astype(np.float32).copy(),
        "ends": np.stack([first, begin], 1).astype(np.float32),
    }


WB = 8
RECIP_BITS = float(0x7E7311C3)
I32 = mybir.dt.int32


def build(nc, x, ctx_in, w1, b1, w2, b2, identity, walk_step, codes_in, ends_in, out):
    with ExitStack() as stack:
        def sb(name, shape, dt=F32):
            return stack.enter_context(nc.sbuf_tensor(name, shape, dt))

        def sem(name):
            return stack.enter_context(nc.semaphore(name))

        big = sb("big", [P, 4 * NF * S])
        xq_store = sb("xq_store", [P, NF * S])
        w1q_store = sb("w1q_store", [P, 2 * Q * S])
        w2q_store = sb("w2q_store", [P, 2 * Q * S])
        ctx_rows = sb("ctx_rows", [P, B, D])
        ybuf = sb("ybuf", [P, 4, 512])
        ident = sb("ident", [P, P])
        identb = sb("identb", [P, P], BF16)
        walk = sb("walk", [P, P], BF16)
        codes = sb("codes", [P, 2 * RW])
        ends = sb("ends", [P, 2])
        stats = sb("stats", [P, 2, Q, 6])
        mv = sb("mv", [P, 2, Q, 2])
        small = sb("small", [P, 2, 7, Q])
        aa = sb("aa", [P, B])
        tiny = sb("tiny", [P, 1])
        magic = sb("magic", [P, 1])
        walked = sb("walked", [P, SK], BF16)
        wcodes = sb("wcodes", [P, 4, SK], BF16)
        span = sb("span", [P, 2, P], BF16)
        codesb = sb("codesb", [P, RW], BF16)
        rmax = sb("rmax", [P, 2, Q])
        part = sb("part", [P, 8])
        ymax = sb("ymax", [P, NT + 4])
        wsc = sb("wsc", [P, 3, 20])
        bcol = sb("bcol", [P, NF + K])
        aff = sb("aff", [P, 6, NF])
        qrow = sb("qrow", [1, 8])
        qsc = sb("qsc", [P, 2, 2])
        onesr = sb("onesr", [1, P])
        hmax = sb("hmax", [P, B * 4 + 6])
        x2_dram = nc.dram_tensor("x2_dram", (B, P, Q, D), F32, kind="Internal").ap()
        h_dram = nc.dram_tensor("h_dram", (4, P, NF * S), F32, kind="Internal").ap()
        cost_dram = nc.dram_tensor("cost_dram", (B, C * (SK + 1) * CW), F32, kind="Internal").ap()
        s2_dram = nc.dram_tensor("s2_dram", (K, P), F32, kind="Internal").ap()
        b2_dram = nc.dram_tensor("b2_dram", (K, P), F32, kind="Internal").ap()

        half = 2 * NF * S
        X = big[:, 0:half].rearrange("p (b q d) -> p b q d", b=B, q=Q)
        Y2T = big[:, half:2 * half].rearrange("p (b k s) -> p b k s", b=B, k=K)
        H = big[:, :].rearrange("p (n f s) -> p n f s", n=4, f=NF)
        o = half
        R = big[:, o:o + (SK + 2) * RW]
        o += (SK + 2) * RW
        M = big[:, o:o + SK * RW]
        o += SK * RW
        COST = big[:, o:o + SK * CW]
        o += SK * CW
        L = big[:, o:o + SK * RW]
        o += SK * RW
        F = big[:, o:o + SK * RW]
        o += SK * RW
        assert o <= 2 * half
        ctxT = F[:, 0:K * B * T].rearrange("p (k n) -> p k n", k=K)
        dist = [z[:, 0:4 * PAD].rearrange("p (n s) -> p n s", n=4) for z in (R, M)]
        bbw = R[:, 4 * PAD:4 * PAD + 2 * Q * T].rearrange("p (n q i) -> p n q i", n=2, q=Q)
        tail = big[:, 2 * half - 2048:2 * half]
        spans = [tail[0:T, 264 * n:264 * n + 264].bitcast(BF16) for n in range(2)]
        both_spans = tail[0:T, 0:528].bitcast(BF16)
        path = [tail[0:T, 528 + 264 * n:792 + 264 * n].bitcast(BF16) for n in range(2)]
        HI, MID, LO = [xq_store[0:T, 2048 * n:2048 * n + 2048].bitcast(BF16).rearrange("p (b d) -> p b d", b=B)
                       for n in range(3)]
        RAW = xq_store[:, :].rearrange("p (n s) -> p n s", n=NF)
        XQ = xq_store[:, :].bitcast(BF16).rearrange("p (b k s) -> p b k s", b=B, k=K)
        XQF = xq_store[:, :].bitcast(BF16)
        HQ = xq_store[:, :].bitcast(BF16).rearrange("p (n f s) -> p n f s", n=2, f=NF)
        Y = w1q_store[:, :].rearrange("p (n q d) -> p n q d", n=2, q=Q)
        YT = w2q_store[:, :].rearrange("p (n k s) -> p n k s", n=2, k=K)
        W1 = w1q_store[:, :].bitcast(BF16).rearrange("p (k f) -> p k f", k=K)
        W2 = w2q_store[:, :].bitcast(BF16).rearrange("p (f d) -> p f d", f=NF)
        XB = w1q_store[:, :].rearrange("p (n q d) -> p n q d", n=2, q=Q)
        s2row = ctx_rows[:, 0, :]
        b2row = ctx_rows[:, 1, :]
        wqb = ybuf[:, :, :].rearrange("p n s -> p (n s)").bitcast(BF16).rearrange("p (n s) -> p n s", n=8)

        def codes_and_ends(b):
            ends_ = span[0:T, :, :].rearrange("p n (c b) -> p n b c", b=B)
            return (codesb[0:T, 1:RW].unsqueeze(1).broadcast_to([T, C, CW]),
                    [ends_[:, n, b, :].unsqueeze(2).broadcast_to([T, C, CW]) for n in range(2)])

        bank = [stack.enter_context(nc.psum_tensor(f"bank{n}", [P, 512], F32)) for n in range(8)]

        vector_step = sem("vector_step")
        ways_on = sem("ways_on")
        w2_part = sem("w2_part")
        small_step = sem("small_step")
        stats_ready = sem("stats_ready")
        context_norms = sem("context_norms")
        root_squared = sem("root_squared")
        correction_ready = sem("correction_ready")
        consts_in = sem("consts_in")
        context_in = [sem(f"context_in{h}") for h in range(2)]
        first_x_in = [sem(f"first_x_in{n}") for n in range(2)]
        x_in = [sem(f"x_in{b}") for b in range(B)]
        weights_in = [sem(f"weights_in{n}") for n in range(3)]
        cost_zeroed = sem("cost_zeroed")
        cost_dram_zeroed = sem("cost_dram_zeroed")
        costs_written = [sem(f"costs_written{n}") for n in range(2)]
        costs_in = sem("costs_in")
        setup_done = sem("setup_done")
        scales_ready = sem("scales_ready")
        context_turned = sem("context_turned")
        context_copied = sem("context_copied")
        variance_ready = sem("variance_ready")
        deviation_ready = sem("deviation_ready")
        y_ready = sem("y_ready")
        y_turned = sem("y_turned")
        y_copied = sem("y_copied")
        half_squares = sem("half_squares")
        products_ready = sem("products_ready")
        squares_ready = sem("squares_ready")
        root_ready = sem("root_ready")
        recip_ready = sem("recip_ready")
        costs_ready = sem("costs_ready")
        last_costs_ready = sem("last_costs_ready")
        rest_ready = sem("rest_ready")
        weights_scaled = sem("weights_scaled")
        weights_rounded = sem("weights_rounded")
        weights_turned = sem("weights_turned")
        weights_copied = sem("weights_copied")
        dtw_step = sem("dtw_step")
        looked_up = sem("looked_up")
        walk_stepped = sem("walk_stepped")
        pieces_ready = sem("pieces_ready")
        pieces_turned = sem("pieces_turned")
        compared = sem("compared")
        path_ready = sem("path_ready")
        ends_moved = sem("ends_moved")
        differences_ready = sem("differences_ready")
        differences_held = sem("differences_held")
        gathered = sem("gathered")
        first_part = sem("first_part")
        first_rest = sem("first_rest")
        second_part = sem("second_part")
        third_part = sem("third_part")
        x2_ready = sem("x2_ready")
        shift_ready = sem("shift_ready")
        y2_ready = sem("y2_ready")
        y2_turned = sem("y2_turned")
        y2_copied = sem("y2_copied")
        x2_spilled = sem("x2_spilled")
        max_ready = sem("max_ready")
        max_turned = sem("max_turned")
        step_ready = sem("step_ready")
        step_spread = sem("step_spread")
        step_copied = sem("step_copied")
        tokens_scaled_odd = sem("tokens_scaled_odd")
        tokens_scaled_even = sem("tokens_scaled_even")
        tokens_rounded = sem("tokens_rounded")
        bias1_ready = sem("bias1_ready")
        layer1_done = sem("layer1_done")
        hidden_ready = sem("hidden_ready")
        hidden_max = sem("hidden_max")
        hidden_spilled = [sem(f"hidden_spilled{n}") for n in range(4)]
        hidden_back = [sem(f"hidden_back{n}") for n in range(4)]
        hidden_scaled = sem("hidden_scaled")
        hidden_rounded = sem("hidden_rounded")
        x2_back = [sem(f"x2_back{n}") for n in range(2)]
        x2_biased = sem("x2_biased")
        layer2_done = sem("layer2_done")
        output_scaled = sem("output_scaled")
        sum_ready = sem("sum_ready")
        last_sum_ready = sem("last_sum_ready")
        out_written = [sem(f"out_written{n}") for n in range(2)]
        w2_scales_out = sem("w2_scales_out")
        w2_scales_row = sem("w2_scales_row")
        biases_in = sem("biases_in")
        bias2_ready = sem("bias2_ready")
        bias2_out = sem("bias2_out")
        bias2_row = sem("bias2_row")

        block = stack.enter_context(nc.Block())

        x_v = x.rearrange("b (q p) d -> b p q d", p=P)
        out_v = out.rearrange("b (q p) d -> b p q d", p=P)
        w1_v = w1.rearrange("(n p) d -> p n d", p=P)
        w2_v = w2.rearrange("(n p) (h f) -> p n h f", p=P, h=4)
        order = [4, 5, 6, 7, 0, 1, 2, 3]
        back = [0, 0, 4, 7, 9, 12, 14, 16, 16]

        @block.sync
        def _(sp):
            for n in range(2):
                sp.dma_start(X[:, 0, 2 * n:2 * n + 2, :], x_v[0][:, 2 * n:2 * n + 2, :]).then_inc(first_x_in[n], 16)
            for dst, src in ((ident[:, :], identity), (ybuf[:, 0, 0:P], walk_step), (codes[:, :], codes_in),
                             (ends[:, :], ends_in)):
                sp.dma_start(dst, src).then_inc(consts_in, 16)

            def load_context(h):
                sp.dma_start(ctx_rows[0:T, 4 * h:4 * h + 4, :],
                             ctx_in[4 * h:4 * h + 4].rearrange("b i d -> i b d")).then_inc(context_in[h], 16)

            load_context(0)

            def load_x(b):
                sp.dma_start(X[:, b, :, :], x_v[b]).then_inc(x_in[b], 16)

            load_x(1)
            load_x(2)
            load_context(1)
            load_x(3)
            sp.dma_start(RAW[:, 0:8, :], w1_v[:, 0:8, :]).then_inc(weights_in[0], 16)
            load_x(4)
            sp.wait_ge(cost_zeroed, 1)
            for b in range(B):
                sp.dma_start(cost_dram[b, 0:C * SK * CW].rearrange("(c t) -> c t", c=C),
                             COST[C * b:C * b + C, :]).then_inc(cost_dram_zeroed, 16)
            sp.dma_start(cost_dram[:, C * SK * CW:].rearrange("b (o n) -> (b o) n", o=1),
                         COST[0:B, 0:C * CW]).then_inc(cost_dram_zeroed, 16)
            load_x(5)
            load_x(6)
            sp.wait_ge(cost_dram_zeroed, 16 * (B + 1))

            def read_costs(b):
                sp.wait_ge(costs_written[b % 2], 16 * (b // 2 + 1))
                sp.dma_start(COST[C * b:C * b + C, :],
                             cost_dram[b, 0:C * SK * CW].rearrange("(c t) -> c t", c=C)).then_inc(costs_in, 16)

            for b in range(B):
                if b < B - 1:
                    sp.wait_ge(costs_ready, b + 1)
                else:
                    sp.wait_ge(last_costs_ready, 1)
                skewed = cost_dram[b].rearrange("(c z) -> c z", c=C)[:, 0:T * CW]
                sp.dma_start(skewed.rearrange("c (i j) -> i c j", j=CW),
                             dist[b % 2][0:T, 3, :].rearrange("i (c j) -> i c j",
                                                              j=CW)).then_inc(costs_written[b % 2], 16)
                if b == 0:
                    load_x(7)
                    with nc.allow_non_contiguous_dma(reason="2048 words, off the critical path"):
                        sp.dma_start(bcol[:, 0:NF], b1.rearrange("(n p) -> p n", p=P)).then_inc(biases_in, 16)
                        sp.dma_start(bcol[:, NF:NF + K], b2.rearrange("(n p) -> p n", p=P)).then_inc(biases_in, 16)
                if b == 1:
                    sp.dma_start(RAW[:, 8:16, :], w1_v[:, 8:16, :]).then_inc(weights_in[1], 16)
                if b >= 1:
                    read_costs(b - 1)
            read_costs(B - 1)
            sp.wait_ge(weights_rounded, NF)
            sp.dma_start(RAW.rearrange("p (n h) s -> p n h s", n=4), w2_v).then_inc(weights_in[2], 16)
            for b in range(B):
                sp.wait_ge(x2_ready, (b + 1) * Q)
                sp.dma_start(x2_dram[b], X[:, b, :, :]).then_inc(x2_spilled, 16)
            sp.wait_ge(w2_scales_out, 16)
            sp.wait_ge(third_part, B)
            sp.dma_start(s2row, s2_dram.rearrange("n (o p) -> o (n p)", o=1).broadcast_to([P,
                         D])).then_inc(w2_scales_row, 16)
            for n in range(4):
                for g in range(4):
                    sp.wait_ge(hidden_ready, n * NF + 4 * g + 4)
                    sp.dma_start(h_dram[n, :, g * 2048:g * 2048 + 2048],
                                 H[:, n, 4 * g:4 * g + 4, :]).then_inc(hidden_spilled[n], 16)

            def come_back(m):
                n, g = m // 4, m % 4
                sp.wait_ge(hidden_rounded, m + 4)
                if g == 0:
                    sp.wait_ge(hidden_spilled[n], 64)
                sp.dma_start(H[:, n, 4 * g:4 * g + 4, :],
                             h_dram[n, :, g * 2048:g * 2048 + 2048]).then_inc(hidden_back[n], 16)

            for i in range(B):
                if i == 0:
                    sp.wait_ge(x2_spilled, 16 * B)
                    sp.wait_ge(layer1_done, B * NF)
                if i >= 2:
                    if i < B - 1:
                        come_back(back[i])
                    sp.wait_ge(out_written[i % 2], 16 * (i // 2))
                sp.dma_start(XB[:, i % 2, :, :], x2_dram[order[i]]).then_inc(x2_back[i % 2], 16)
                if i == 0:
                    sp.wait_ge(bias2_ready, 1)
                    with nc.allow_non_contiguous_dma(reason="512 words"):
                        sp.dma_start(b2_dram.rearrange("n p -> p n"), aff[:, 1, 0:K]).then_inc(bias2_out, 16)
                    sp.wait_ge(bias2_out, 16)
                    sp.dma_start(b2row, b2_dram.rearrange("n (o p) -> o (n p)", o=1)
                                 .broadcast_to([P, D])).then_inc(bias2_row, 16)
                for m in range(back[i] + (2 <= i < B - 1), back[i + 1]):
                    come_back(m)
                if i >= 1:
                    sp.wait_ge(sum_ready, Q * i)
                    sp.dma_start(out_v[order[i - 1]], XB[:, (i - 1) % 2, :, :]).then_inc(out_written[(i - 1) % 2], 16)
            for q in range(Q):
                if q < Q - 1:
                    sp.wait_ge(sum_ready, Q * (B - 1) + q + 1)
                else:
                    sp.wait_ge(last_sum_ready, 1)
                sp.dma_start(out_v[order[B - 1]][:, q, :], XB[:, (B - 1) % 2, q,
                             :]).then_inc(out_written[(B - 1) % 2], 16)
            sp.wait_ge(out_written[0], 16 * B // 2)
            sp.wait_ge(out_written[1], 16 * (B // 2 - 1 + Q))

        @block.gpsimd
        def _(pool):
            g = nc.gpsimd
            g.memset(COST, 0.0).then_inc(cost_zeroed, 1)
            g.memset(tiny[:, :], 1e-30).then_inc(setup_done, 1)
            g.memset(onesr[:, :], 1.0).then_inc(setup_done, 1)
            g.memset(magic[:, :], MAGIC).then_inc(setup_done, 1)
            for n in range(2):
                g.memset(dist[n][0:T, 3, S:PAD], BIG).then_inc(setup_done, 1)
            pool.wait_ge(consts_in, 64)
            g.tensor_copy(identb[:, :], ident[:, :]).then_inc(setup_done, 1)
            g.tensor_copy(walk[:, :], ybuf[:, 0, 0:P]).then_inc(setup_done, 1)
            g.tensor_copy(codesb[:, :], codes[:, 0:RW]).then_inc(setup_done, 1)
            pool.wait_ge(setup_done, 8)
            for b in range(B - 1):
                t = dist[b % 2][0:T]
                pool.wait_ge(root_squared, b + 1)
                g.tensor_tensor(t[:, 2, 0:S], t[:, 0, 0:S], t[:, 2, 0:S], ALU.subtract).then_inc(rest_ready, 1)
                pool.wait_ge(rest_ready, b + 1)
                pool.wait_ge(recip_ready, b + 1)
                g.tensor_tensor(t[:, 2, 0:S], t[:, 2, 0:S], t[:, 3, 0:S], ALU.mult).then_inc(correction_ready, 1)
                pool.wait_ge(correction_ready, b + 1)
                g.tensor_tensor(t[:, 3, 0:S], t[:, 1, 0:S], t[:, 2, 0:S], ALU.add).then_inc(costs_ready, 1)
            for n in range(2 * NF):
                pool.wait_ge(weights_scaled, n + 1)
                if n >= 8:
                    pool.wait_ge(weights_turned, n - 7)
                g.tensor_scalar(wqb[:, n % 8, :], RAW[:, n % NF, :], -MAGIC, 1.0, ALU.add,
                                ALU.mult).then_inc(weights_rounded, 1)
                if n in (NF + 3, NF + 7):
                    for b in range(n - NF - 3, n - NF + 1):
                        pool.wait_ge(first_part, b + 1)
                        g.tensor_tensor(ctx_rows[0:T, b, :], ctx_rows[0:T, b, :], HI[:, b, :],
                                        ALU.subtract).then_inc(first_rest, 1)
                if n in (NF + 11, NF + 15):
                    pool.wait_ge(weights_rounded, NF + 12)
                    for b in range(n - NF - 11, n - NF - 7):
                        pool.wait_ge(second_part, b + 1)
                        g.tensor_tensor(LO[:, b, :], ctx_rows[0:T, b, :], MID[:, b, :],
                                        ALU.subtract).then_inc(third_part, 1)
            for b in range(1, B):
                if b == 1:
                    pool.wait_ge(compared, 2)
                else:
                    pool.wait_ge(path_ready, b)
                    if b == 2:
                        pool.wait_ge(ends_moved, 1)
                    c3, sp3 = codes_and_ends(b)
                    s3 = [z.rearrange("p (c j) -> p c j", c=C) for z in spans]
                    g.tensor_tensor(s3[0], c3, sp3[0], ALU.subtract).then_inc(differences_ready, 1)
                    g.tensor_tensor(s3[1], sp3[1], c3, ALU.subtract).then_inc(differences_ready, 1)
                    pool.wait_ge(differences_held, b - 1)
                    pool.wait_ge(gathered, Q * (b - 1))
                g.tensor_tensor(path[b % 2], spans[0], spans[1], ALU.mult).then_inc(path_ready, 1)
            pool.wait_ge(step_copied, 1)
            for b in range(0, B, 2):
                pool.wait_ge(y2_copied, (b + 1) * K)
                for k in range(K):
                    ins = g.tensor_scalar(Y2T[:, b, k, :], Y2T[:, b, k, :], qsc[:, 0, 1:2], MAGIC, ALU.mult, ALU.add)
                ins.then_inc(tokens_scaled_even, 1)
            pool.wait_ge(bias2_row, 16)

            def finish(pair, odd, tiles):
                pool.wait_ge(x2_back[odd], (pair + 1) * 16)
                for q in range(Q):
                    g.tensor_tensor(XB[:, odd, q, :], XB[:, odd, q, :], b2row, ALU.add).then_inc(x2_biased, 1)
                for q in range(tiles):
                    n = pair * (2 * Q) + (odd * Q + q)
                    pool.wait_ge(x2_biased, n + 1)
                    pool.wait_ge(output_scaled, n + 1)
                    g.tensor_tensor(XB[:, odd, q, :], XB[:, odd, q, :], ybuf[:, q, :], ALU.add).then_inc(sum_ready, 1)

            with pool.Fori(0, B // 2 - 1) as pair:
                finish(pair, 0, Q)
                finish(pair, 1, Q)
            finish(B // 2 - 1, 0, Q)
            finish(B // 2 - 1, 1, Q - 1)

        @block.scalar
        def _(act):
            a = nc.scalar
            ID = ACT.Identity

            def root(n, wait):
                act.wait_ge(variance_ready, wait)
                a.activation(small[:, n % 2, 1, :], small[:, n % 2, 0, :], ACT.Sqrt).then_inc(deviation_ready, 1)

            def costs(b):
                t = dist[b % 2][0:T]
                act.wait_ge(context_norms, b + 1)
                act.wait_ge(products_ready, b + 1)
                if b >= 2:
                    act.wait_ge(costs_ready, b - 1)
                a.activation(t[:, 0, 0:S], bank[4 + b % 2][0:T, :], ACT.Relu, bias=aa[0:T, b:b + 1],
                             scale=-2.0).then_inc(squares_ready, 1)
                act.wait_ge(squares_ready, b + 1)
                a.activation(t[:, 1, 0:S], t[:, 0, 0:S], ACT.Sqrt, bias=tiny[0:T, :]).then_inc(root_ready, 1)
                act.wait_ge(root_ready, b + 1)
                a.activation(t[:, 2, 0:S], t[:, 1, 0:S], ACT.Square).then_inc(root_squared, 1)

            root(0, 1)

            def context_out(h):
                for k in range(K):
                    act.wait_ge(context_turned, h * K + k + 1)
                    a.activation(ctxT[:, k, 4 * T * h:4 * T * h + 4 * T], bank[k][:, 0:4 * T],
                                 ID).then_inc(context_copied, 1)

            context_out(0)
            act.wait_ge(setup_done, 8)
            for b in range(B):
                if b >= 2:
                    act.wait_ge(products_ready, b - 1)
                for k in range(K):
                    act.wait_ge(y_turned, b * K + k + 1)
                    a.activation(YT[:, b % 2, k, :], bank[k][:, :], ID).then_inc(y_copied, 1)
                if b == 0:
                    root(1, 2)
                    context_out(1)
                if b >= 2:
                    act.wait_ge(context_norms, b - 1)
                a.activation(ybuf[0:T, 1 + b % 2, :], ctx_rows[0:T, b, :], ACT.Square,
                             accum_out=aa[0:T, b:b + 1]).then_inc(context_norms, 1)
                if b >= 1:
                    costs(b - 1)
                if b + 2 < B:
                    root(b, b + 3)
            costs(B - 1)

            def weights(n):
                if n >= NF and n % 4 == 0:
                    act.wait_ge(scales_ready, 2 + (n - NF) // 4)
                col = n if n < NF else NF + (n - NF) // 4
                a.activation(RAW[:, n % NF, :], RAW[:, n % NF, :], ID, bias=magic[:, :],
                             scale=wsc[:, 2, col:col + 1]).then_inc(weights_scaled, 1)

            def turned(m):
                act.wait_ge(weights_turned, m + 1)
                src = bank[m % 4][:, 0:256].bitcast(BF16).rearrange("p (k f) -> p k f", k=4)
                if m < NF:
                    dst = W1[:, :, m * P:m * P + P]
                else:
                    dt_, h = (m - NF) // 4, (m - NF) % 4
                    dst = W2[:, 4 * h:4 * h + 4, dt_ * P:dt_ * P + P]
                a.activation(dst, src, ID).then_inc(weights_copied, 1)

            act.wait_ge(scales_ready, 1)
            for n in range(NF + 2):
                if n < NF:
                    weights(n)
                if n >= 2:
                    turned(n - 2)
            for t in range(5):
                if t < 4:
                    for n in range(NF + 4 * t, NF + 4 * t + 4):
                        weights(n)
                if t == 0:
                    act.wait_ge(weights_rounded, NF + 4)
                    for b in range(B):
                        a.activation(HI[:, b, :], ctx_rows[0:T, b, :], ID).then_inc(first_part, 1)
                else:
                    for n in range(NF + 4 * t - 4, NF + 4 * t):
                        turned(n)
                if t == 1:
                    act.wait_ge(weights_rounded, NF + 8)
                    for b in range(B):
                        act.wait_ge(first_rest, b + 1)
                        a.activation(MID[:, b, :], ctx_rows[0:T, b, :], ID).then_inc(second_part, 1)

            with nc.allow_non_contiguous_dma(reason="512 words, off the critical path"):
                act.dma_start(s2_dram.rearrange("n p -> p n"), wsc[:, 1, NF:NF + 4]).then_inc(w2_scales_out, 16)

            def tokens_up(b):
                a.activation(Y2T[:, b, :, :], Y2T[:, b, :, :], ID, bias=magic[:, :],
                             scale=qsc[:, 0, 1:2]).then_inc(tokens_scaled_odd, 1)

            root(0, B + 1)
            for b in range(B):
                act.wait_ge(shift_ready, b + 1)
                if b >= 1:
                    act.wait_ge(y2_turned, K * b)
                for q in range(Q):
                    a.activation(ybuf[:, q, :], X[:, b, q, :], ID, bias=small[:, b % 2, 6, q:q + 1],
                                 scale=small[:, b % 2, 5, q:q + 1]).then_inc(y2_ready, 1)
                    if q == 1 and b + 1 < B:
                        root(b + 1, B + b + 2)
                for k in range(K):
                    act.wait_ge(y2_turned, b * K + k + 1)
                    a.activation(Y2T[:, b, k, :], bank[k][:, :], ID).then_inc(y2_copied, 1)

            act.wait_ge(y2_copied, B * K)
            act.wait_ge(step_copied, 1)
            tokens_up(1)
            act.wait_ge(bias1_ready, 1)
            act.wait_ge(x2_spilled, 16 * B)
            for n in range(B):
                if n == 2:
                    act.wait_ge(tokens_rounded, B)
                for f in range(NF):
                    if n >= 4 and f == 0:
                        act.wait_ge(hidden_spilled[n - 4], 64)
                    act.wait_ge(layer1_done, n * NF + f + 1)
                    if n >= 4 and f % 4 == 0:
                        act.wait_ge(hidden_max, (n - 4) * 4 + f // 4 + 1)
                    a.activation(H[:, n % 4, f, :], bank[(f + 4) % 8][:, :], ACT.Relu, bias=aff[:, 1, f:f + 1],
                                 scale=aff[:, 0, f:f + 1]).then_inc(hidden_ready, 1)
                    if n * NF + f in (3, 11, 19):
                        tokens_up(3 + 2 * ((n * NF + f) // 8))
            act.wait_ge(step_copied, 2)
            for i in range(B):
                for g in range(4):
                    if i >= 4:
                        act.wait_ge(hidden_back[i - 4], 64)
                    for f, m in [(f, 1) for f in range(4)] if i + g == 0 else [(4 * g, 4)]:
                        a.activation(H[:, i % 4, f:f + m, :], H[:, i % 4, f:f + m, :], ID,
                                     bias=magic[:, :], scale=qsc[:, 1, 1:2]).then_inc(hidden_scaled, 1)

        @block.vector
        def _(dve):
            v = nc.vector
            chain = [0]

            def link(ins):
                chain[0] += 1
                ins.then_inc(vector_step, 1)
                dve.wait_ge(vector_step, chain[0])

            smalls = [0]

            def small_done(ins):
                smalls[0] += 1
                ins.then_inc(small_step, 1)

            def after_small():
                dve.wait_ge(small_step, smalls[0])

            def rsqrt_step(b, n):
                m = small[:, b % 2]
                after_small()
                if n == 0:
                    small_done(v.reciprocal(m[:, 2, :], m[:, 1, :]))
                elif n == 1:
                    small_done(v.tensor_tensor(m[:, 3, :], m[:, 2, :], m[:, 2, :], ALU.mult))
                elif n == 2:
                    small_done(v.tensor_tensor(m[:, 3, :], m[:, 3, :], m[:, 0, :], ALU.mult))
                elif n == 3:
                    small_done(v.tensor_scalar(m[:, 3, :], m[:, 3, :], -0.5, 1.5, ALU.mult, ALU.add))
                else:
                    small_done(v.tensor_tensor(m[:, 5, :], m[:, 2, :], m[:, 3, :], ALU.mult))

            def variance(b, n):
                dve.wait_ge(stats_ready, n)
                for q in range(Q):
                    v.bn_aggr(mv[:, b % 2, q, :], stats[:, b % 2, q, :]).then_inc(small_step, 1)
                smalls[0] += Q
                after_small()
                v.tensor_scalar(small[:, b % 2, 0, :], mv[:, b % 2, :, 1], EPS_LN, None,
                                ALU.add).then_inc(variance_ready, 1)

            def w1_max(n):
                if n % 8 == 0:
                    dve.wait_ge(weights_in[n // 8], 16)
                v.tensor_reduce(wsc[:, 0, n:n + 1], RAW[:, n, :], AX, ALU.max,
                                apply_absolute_value=True).then_inc(vector_step, 1)
                chain[0] += 1

            def normalized(p):
                m = small[:, p % 2]
                if p >= 2:
                    dve.wait_ge(y_turned, K * (p - 1))
                for q in range(Q):
                    v.tensor_scalar(Y[:, p % 2, q, :], X[:, p, q, :], mv[:, p % 2, q, 0:1], m[:, 5, q:q + 1],
                                    ALU.subtract, ALU.mult).then_inc(y_ready, 1)
                after_small()
                small_done(v.tensor_tensor(m[:, 4, :], m[:, 4, :], mv[:, p % 2, :, 1], ALU.mult))

            def rsqrt_end(p):
                m = small[:, p % 2]
                rsqrt_step(p, 4)
                after_small()
                small_done(v.tensor_tensor(m[:, 4, :], m[:, 5, :], m[:, 5, :], ALU.mult))

            def half_square(p):
                m = small[:, p % 2]
                after_small()
                if p >= 2:
                    dve.wait_ge(products_ready, p - 1)
                v.tensor_scalar(bbw[:, p % 2, :, :], m[:, 4, :].unsqueeze(2).broadcast_to([P, Q, T]), -0.5 * D,
                                None, ALU.mult).then_inc(half_squares, 1)

            for b in range(B + 4):
                p = b - 1
                if 1 <= b < B:
                    dve.wait_ge(x_in[b], 16)
                for q in range(Q):
                    if b == 0 and q % 2 == 0:
                        dve.wait_ge(first_x_in[q // 2], 16)
                    if b < B:
                        v.bn_stats(stats[:, b % 2, q, :], X[:, b, q, :]).then_inc(stats_ready, 1)
                    if 1 <= p < B:
                        if q == 0:
                            dve.wait_ge(deviation_ready, p + 1)
                        rsqrt_step(p, q)
                if 1 <= p < B:
                    rsqrt_end(p)
                if b < B:
                    variance(b, Q * (b + 1))
                if b == 0:
                    dve.wait_ge(deviation_ready, 1)
                    for q in range(Q):
                        rsqrt_step(0, q)
                    rsqrt_end(0)
                    normalized(0)
                    half_square(0)
                if 1 <= p < B:
                    normalized(p)
                for n in {3: [0], 4: [1], 5: [2], 6: [3], 8: [4], 9: range(5, 12)}.get(b, []):
                    w1_max(n)
                if 1 <= p < B:
                    half_square(p)
                if b - 3 >= 0 and b - 3 < B:
                    n = b - 3
                    t = dist[n % 2][0:T]
                    dve.wait_ge(root_ready, n + 1)
                    if n >= 2:
                        dve.wait_ge(costs_written[n % 2], 16 * (n // 2))
                    v.tensor_scalar(t[:, 3, 0:S].bitcast(I32), t[:, 1, 0:S].bitcast(I32), -1.0, RECIP_BITS, ALU.mult,
                                    ALU.add).then_inc(recip_ready, 1)
                if b - 3 == B - 1:
                    dve.wait_ge(root_squared, B)
                    dve.wait_ge(recip_ready, B)
                    link(v.tensor_tensor(t[:, 2, 0:S], t[:, 0, 0:S], t[:, 2, 0:S], ALU.subtract))
                    link(v.tensor_tensor(t[:, 2, 0:S], t[:, 2, 0:S], t[:, 3, 0:S], ALU.mult))
                    v.tensor_tensor(t[:, 3, 0:S], t[:, 1, 0:S], t[:, 2, 0:S], ALU.add).then_inc(last_costs_ready, 1)
            for n in range(12, NF):
                w1_max(n)
            dve.wait_ge(vector_step, chain[0])
            link(v.tensor_scalar(wsc[:, 1, 0:NF], wsc[:, 0, 0:NF], EPS_Q, 1.0 / 127.0, ALU.max, ALU.mult))
            v.reciprocal(wsc[:, 2, 0:NF], wsc[:, 1, 0:NF]).then_inc(scales_ready, 1)

            def row(t, a, n):
                return R[:, t * RW + a:t * RW + a + n]

            left = [C * (i // C) + (i % C - 1) % C for i in range(32)]
            for n in range(2):
                dve.wait_ge(costs_written[n], 16 * B // 2)
            link(v.memset(R[:, 0:2 * RW], BIG))
            link(v.tensor_copy(R[:, 0:1], ends[:, 0:1]))
            L3 = L.rearrange("p (t j) -> p t j", j=RW)
            F3 = F.rearrange("p (t j) -> p t j", j=RW)
            v.memset(L3[:, :, 0:1], 0.0).then_inc(vector_step, 1)
            v.memset(F3[:, :, 0:1], OUT).then_inc(vector_step, 1)
            chain[0] += 2
            v.tensor_tensor(M[:, 0:CW], row(0, 1, CW), row(0, 0, CW), ALU.min).then_inc(dtw_step, 1)
            dve.wait_ge(costs_in, 16 * B)
            for t in range(SK):
                dve.wait_ge(dtw_step, 1 + 3 * t)
                v.tensor_tensor_scan(row(t + 1, 1, CW), M[:, t * CW:t * CW + CW], COST[:, t * CW:t * CW + CW],
                                     row(t + 1, 0, 1), ALU.min, ALU.add).then_inc(dtw_step, 1)
                v.tensor_tensor(F3[:, t, 1:RW], row(t, 0, CW), row(t, 1, CW), ALU.is_le).then_inc(vector_step, 1)
                dve.wait_ge(dtw_step, 2 + 3 * t)
                if t + 1 < SK:
                    v.tensor_tensor(M[:, (t + 1) * CW:(t + 2) * CW], row(t + 1, 1, CW), row(t + 1, 0, CW),
                                    ALU.min).then_inc(dtw_step, 1)
                    v.stream_shuffle(row(t + 2, 0, 1), row(t + 1, CW, 1), left).then_inc(dtw_step, 1)
                v.tensor_tensor(L3[:, t, 1:RW], row(t + 1, 0, CW), M[:, t * CW:t * CW + CW],
                                ALU.is_lt).then_inc(vector_step, 1)
            chain[0] += 2 * SK
            dve.wait_ge(vector_step, chain[0])

            N3 = M.rearrange("p (t j) -> p t j", j=RW)

            def way_on(k, n):
                e = SK - k * WB
                a = max(e - WB, 0)
                if e <= 0:
                    return
                if n == 0:
                    v.scalar_tensor_tensor(out=F3[:, a:e, 1:RW], in0=F3[:, a:e, 1:RW], scalar=DIAG + 1,
                                           in1=codes[:, 1:RW].unsqueeze(1).broadcast_to([P, e - a, CW]),
                                           op0=ALU.mult, op1=ALU.add).then_inc(ways_on, 1)
                elif n == 1:
                    dve.wait_ge(ways_on, 3 * k + 1)
                    v.scalar_tensor_tensor(out=F3[:, a:e, 1:RW], in0=L3[:, a:e, 1:RW], scalar=0.0,
                                           in1=F3[:, a:e, 1:RW], op0=ALU.is_equal, op1=ALU.mult).then_inc(ways_on, 1)
                else:
                    dve.wait_ge(ways_on, 3 * k + 2)
                    v.tensor_tensor_scan(M[:, a * RW:e * RW], L[:, a * RW:e * RW], F[:, a * RW:e * RW], OUT,
                                         ALU.mult, ALU.add).then_inc(ways_on, 1)

            def w2_max(j):
                n, i = j // 11, j % 11
                if n >= K:
                    return
                col = wsc[:, :, NF + n:NF + n + 1]
                if j == 0:
                    dve.wait_ge(weights_in[2], 16)
                if i < 8:
                    if i == 0 and n:
                        dve.wait_ge(w2_part, 10 * n)
                    v.tensor_reduce(part[:, i:i + 1], RAW[:, 4 * n + i // 2, 256 * (i % 2):256 * (i % 2) + 256], AX,
                                    ALU.max, apply_absolute_value=True).then_inc(w2_part, 1)
                elif i == 8:
                    dve.wait_ge(w2_part, 10 * n + 8)
                    v.tensor_reduce(col[:, 0, :], part[:, :], AX, ALU.max).then_inc(w2_part, 1)
                elif i == 9:
                    dve.wait_ge(w2_part, 10 * n + 9)
                    v.tensor_scalar(col[:, 1, :], col[:, 0, :], EPS_Q, 1.0 / 127.0, ALU.max,
                                    ALU.mult).then_inc(w2_part, 1)
                else:
                    dve.wait_ge(w2_part, 10 * n + 10)
                    v.reciprocal(col[:, 2, :], col[:, 1, :]).then_inc(scales_ready, 1)

            for n in range(3):
                way_on(0, n)

            both = codes[:, :].rearrange("p (n j) -> p n j", n=2)
            junk = COST[:, 0:2 * RW].rearrange("p (n j) -> p n j", n=2)
            for n in range(SK):
                t = SK - 1 - n
                if n:
                    dve.wait_ge(walk_stepped, n)
                if n % WB == 0:
                    dve.wait_ge(ways_on, 3 * (n // WB) + 3)
                at = ends[:, 1:2] if n == 0 else bank[6][:, t:t + 1]
                v.scalar_tensor_tensor(out=junk, in0=both, scalar=at,
                                       in1=N3[:, t, :].unsqueeze(1).broadcast_to([P, 2, RW]), op0=ALU.is_equal,
                                       op1=ALU.mult, accum_out=walked[:, t:t + 1]).then_inc(looked_up, 1)
                if n % WB < 3:
                    way_on(n // WB + 1, n % WB)
                else:
                    w2_max((WB - 3) * (n // WB) + n % WB - 3)
            dve.wait_ge(looked_up, SK)
            link(v.tensor_copy(wcodes[:, 0, SK - 1:SK], ends[:, 1:2]))
            link(v.tensor_copy(wcodes[:, 0, 0:SK - 1], bank[6][:, 0:SK - 1]))
            link(v.tensor_scalar(wcodes[:, 1, :], wcodes[:, 0, :], DIAG + 0.5, -DIAG, ALU.is_ge, ALU.mult))
            link(v.tensor_tensor(wcodes[:, 2, :], wcodes[:, 0, :], wcodes[:, 1, :], ALU.add))
            link(v.tensor_scalar(wcodes[:, 1, :], walked[:, :], DIAG + 0.5, -DIAG - 1, ALU.is_ge, ALU.mult))
            v.tensor_tensor(wcodes[:, 3, :], walked[:, :], wcodes[:, 1, :], ALU.add).then_inc(pieces_ready, 1)
            dve.wait_ge(pieces_turned, 1)
            link(v.tensor_copy(span[0:T, :, :], bank[7][0:T, 0:2 * P].rearrange("p (n c) -> p n c", n=2)))

            def on_path(b):
                c3, sp3 = codes_and_ends(b)
                if b >= 1:
                    dve.wait_ge(path_ready, b)
                for n, op in ((0, ALU.is_ge), (1, ALU.is_le)):
                    ins = v.tensor_tensor(spans[n].rearrange("p (c j) -> p c j", c=C), c3, sp3[n], op)
                ins.then_inc(compared, 1)

            on_path(0)
            dve.wait_ge(compared, 1)
            v.tensor_tensor(path[0], spans[0], spans[1], ALU.mult).then_inc(path_ready, 1)
            on_path(1)
            dve.wait_ge(compared, 2)
            link(v.tensor_scalar(span[0:T, 0, :], span[0:T, 0, :], -1.0, None, ALU.add))
            v.tensor_scalar(span[0:T, 1, :], span[0:T, 1, :], 1.0, None, ALU.add).then_inc(ends_moved, 1)
            for b in range(B + 1):
                p = b - 1
                m = small[:, p % 2]
                for q in range(Q):
                    n = b * Q + q
                    if b < B:
                        dve.wait_ge(gathered, n + 1)
                        v.tensor_tensor_reduce(X[:, b, q, :], bank[4 + n % 4][:, :], X[:, b, q, :], 1.0, -3.0e38,
                                               ALU.add, ALU.max, rmax[:, b % 2, q:q + 1]).then_inc(x2_ready, 1)
                    if p >= 0:
                        if q == 0:
                            dve.wait_ge(deviation_ready, B + p + 1)
                        rsqrt_step(p, q)
                for q in range(Q):
                    if b < B:
                        dve.wait_ge(x2_ready, b * Q + q + 1)
                        v.bn_stats(stats[:, b % 2, q, :], X[:, b, q, :]).then_inc(stats_ready, 1)
                    if p >= 0 and q == 0:
                        if p >= 2:
                            dve.wait_ge(y2_ready, Q * (p - 1))
                        rsqrt_step(p, 4)
                    elif p >= 0 and q == 1:
                        after_small()
                        v.scalar_tensor_tensor(out=m[:, 6, :], in0=mv[:, p % 2, :, 0], scalar=-1.0, in1=m[:, 5, :],
                                               op0=ALU.mult, op1=ALU.mult).then_inc(shift_ready, 1)
                        small_done(v.tensor_tensor(m[:, 4, :], rmax[:, p % 2, :], mv[:, p % 2, :, 0], ALU.subtract))
                    elif p >= 0 and q == 2:
                        after_small()
                        small_done(v.tensor_tensor(ymax[:, p * Q:p * Q + Q], m[:, 4, :], m[:, 5, :], ALU.mult))
                if b < B:
                    variance(b, Q * (B + b + 1))
                if b + 2 < B:
                    dve.wait_ge(differences_ready, 2 * b + 2)
                    v.tensor_scalar(both_spans, both_spans, 1.0, 0.0, ALU.min, ALU.max).then_inc(differences_held, 1)
            after_small()

            def step_size(n, src):
                v.tensor_reduce(ymax[:, NT + n:NT + n + 1], src, AX, ALU.max).then_inc(max_ready, 1)
                dve.wait_ge(max_turned, n + 1)
                link(v.tensor_reduce(qrow[:, 0:1], bank[7][0:1, 0:P], AX, ALU.max))
                link(v.tensor_scalar(qrow[:, 1:2], qrow[:, 0:1], EPS_Q, 1.0 / 255.0, ALU.max, ALU.mult))
                v.reciprocal(qrow[:, 2:3], qrow[:, 1:2]).then_inc(step_ready, 1)
                dve.wait_ge(step_spread, n + 1)
                v.tensor_copy(qsc[:, n, :], bank[6][:, 0:2]).then_inc(step_copied, 1)
                dve.wait_ge(step_copied, n + 1)

            def on_grid(dst, bias, scale, t, done):
                link(v.reciprocal(t[0], scale))
                link(v.tensor_tensor(t[0], bias, t[0], ALU.mult))
                link(v.scalar_tensor_tensor(out=t[1], in0=t[0], scalar=-1.0, in1=t[0], op0=ALU.mult, op1=ALU.max))
                link(v.tensor_scalar(t[2], t[1], TWO23, TWO23, ALU.add, ALU.subtract))
                link(v.tensor_tensor(t[3], t[1], t[2], ALU.subtract))
                link(v.scalar_tensor_tensor(out=t[3], in0=t[1], scalar=TWO23, in1=t[3], op0=ALU.is_ge, op1=ALU.mult))
                link(v.tensor_tensor(t[2], t[2], t[3], ALU.add))
                link(v.tensor_scalar(t[0], t[0], 0.0, 2.0, ALU.is_ge, ALU.mult))
                link(v.scalar_tensor_tensor(out=t[2], in0=t[0], scalar=-1.0, in1=t[2], op0=ALU.add, op1=ALU.mult))
                v.tensor_tensor(dst, t[2], scale, ALU.mult).then_inc(done, 1)

            step_size(0, ymax[:, 0:NT])

            def tokens_down(b):
                dve.wait_ge(tokens_scaled_odd if b % 2 else tokens_scaled_even, b // 2 + 1)
                v.tensor_scalar(XQ[:, b, :, :], Y2T[:, b, :, :], MAGIC, 0.0, ALU.subtract,
                                ALU.max).then_inc(tokens_rounded, 1)

            link(v.tensor_scalar(aff[:, 0, :], wsc[:, 1, 0:NF], qsc[:, 0, 0:1], None, ALU.mult))
            dve.wait_ge(biases_in, 32)
            on_grid(aff[:, 1, :], bcol[:, 0:NF], aff[:, 0, :], [aff[:, 2 + i, :] for i in range(4)], bias1_ready)
            dve.wait_ge(weights_turned, 2 * NF)
            for b in range(B):
                tokens_down(b)
            for start, groups in ((0, 16), (16, 14)):
                with dve.Fori(0, groups) as n:
                    dve.wait_ge(hidden_ready, n * 4 + (4 * start + 4))
                    v.tensor_reduce(hmax[:, bass.ds(n + start, 1)], big[:, bass.ds(n * (4 * S), 4 * S)], AX,
                                    ALU.max).then_inc(hidden_max, 1)
            for f in range(NF - 8, NF):
                dve.wait_ge(hidden_ready, (B - 1) * NF + f + 1)
                n = B * 4 - 2 + f - (NF - 8)
                v.tensor_reduce(hmax[:, n:n + 1], H[:, (B - 1) % 4, f, :], AX, ALU.max).then_inc(hidden_max, 1)
            dve.wait_ge(hidden_max, B * 4 + 6)
            step_size(1, hmax[:, :])

            def hidden(i):
                for g in range(4):
                    if i >= 2 and g == 0:
                        dve.wait_ge(layer2_done, Q * (i - 1))
                    for f, m in [(f, 1) for f in range(4)] if i + g == 0 else [(4 * g, 4)]:
                        dve.wait_ge(hidden_scaled, f + 1 if m == 1 else 4 * i + g + 4)
                        v.tensor_scalar(HQ[:, i % 2, f:f + m, :], H[:, i % 4, f:f + m, :], MAGIC, 255.0,
                                        ALU.subtract, ALU.min).then_inc(hidden_rounded, 1)
                    if i + g == 0:
                        link(v.tensor_scalar(aff[:, 0, 0:K], wsc[:, 1, NF:NF + K], qsc[:, 1, 0:1], None, ALU.mult))
                        on_grid(aff[:, 1, 0:K], bcol[:, NF:NF + K], aff[:, 0, 0:K],
                                [aff[:, 2 + i, 0:K] for i in range(4)], bias2_ready)

            hidden(0)
            dve.wait_ge(w2_scales_row, 16)
            link(v.tensor_scalar(s2row, s2row, qsc[:, 1, 0:1], None, ALU.mult))
            for i in range(B):
                if i + 1 < B:
                    hidden(i + 1)
                for q in range(Q):
                    n = i * Q + q
                    dve.wait_ge(layer2_done, n + 1)
                    if n >= 4:
                        dve.wait_ge(sum_ready, n - 3)
                    v.tensor_tensor(ybuf[:, q, :], bank[n % 8][:, :], s2row, ALU.mult).then_inc(output_scaled, 1)
            dve.wait_ge(output_scaled, NT)
            dve.wait_ge(x2_biased, NT)
            v.tensor_tensor(XB[:, (B - 1) % 2, Q - 1, :], XB[:, (B - 1) % 2, Q - 1, :], ybuf[:, Q - 1, :],
                            ALU.add).then_inc(last_sum_ready, 1)

        @block.tensor
        def _(pe):
            t = nc.tensor
            pe.wait_ge(consts_in, 64)

            def turn_context(h):
                pe.wait_ge(context_in[h], 16)
                for k in range(K):
                    if h == 1:
                        pe.wait_ge(y_copied, k + 1)
                    for j in range(4):
                        last = t.transpose(bank[k][:, T * j:T * j + T],
                                           ctx_rows[0:T, 4 * h + j, k * P:k * P + P], ident[0:T, 0:T])
                    last.then_inc(context_turned, 1)

            def turn(b):
                for k in range(K):
                    if b <= 1:
                        pe.wait_ge(context_copied, b * K + k + 1)
                    else:
                        pe.wait_ge(y_copied, (b - 1) * K + k + 1)
                    for q in range(Q):
                        if k == 0:
                            pe.wait_ge(y_ready, b * Q + q + 1)
                        last = t.transpose(bank[k][:, q * P:q * P + P], Y[:, b % 2, q, k * P:k * P + P], ident[:, :])
                    last.then_inc(y_turned, 1)

            def distances(b):
                d = bank[4 + b % 2][0:T, :]
                if b >= 2:
                    pe.wait_ge(squares_ready, b - 1)
                for k in range(K):
                    if k == K - 1:
                        pe.wait_ge(half_squares, b + 1)
                        for q in range(Q):
                            t.matmul(d[:, q * P:q * P + P], bbw[:, b % 2, q, :], ident[:, :], start=False, stop=False)
                    pe.wait_ge(y_copied, b * K + k + 1)
                    pe.wait_ge(context_copied, (b // 4) * K + k + 1)
                    last = t.matmul(d, ctxT[:, k, b * T:b * T + T], YT[:, b % 2, k, :], start=(k == 0),
                                    stop=(k == K - 1))
                last.then_inc(products_ready, 1)

            turn_context(0)
            for b in range(B):
                turn(b)
                distances(b)
                if b == 0:
                    turn_context(1)

            def turn_weights(n, k):
                if k == 0:
                    pe.wait_ge(weights_rounded, n + 1)
                    if n == 0:
                        pe.wait_ge(y_copied, B * K)
                    if n >= 4:
                        pe.wait_ge(weights_copied, n - 3)
                ins = t.transpose(bank[n % 4][:, 64 * k:64 * k + 64].bitcast(BF16), wqb[:, n % 8, k * P:k * P + P],
                                  identb[:, :])
                if k == 3:
                    ins.then_inc(weights_turned, 1)

            for n in range(NF):
                for k in range(4):
                    turn_weights(n, k)

            for n in range(SK - 1):
                c = SK - 1 - n
                pe.wait_ge(looked_up, n + 1)
                t.matmul(bank[6][:, c - 1:c], walk[:, :], walked[:, c:c + 1], start=True,
                         stop=True).then_inc(walk_stepped, 1)
                if n >= 31:
                    turn_weights(NF + (n - 31) // 4, (n - 31) % 4)
            for j in range(SK - 1 - 31, 4 * NF):
                turn_weights(NF + j // 4, j % 4)

            pe.wait_ge(pieces_ready, 1)
            for n in range(2):
                for c in range(C):
                    last = t.matmul(bank[7][0:T, n * P + c * B:n * P + c * B + B], wcodes[:, 2 + n, c:c + T],
                                    identb[:, c:c + C * (B - 1) + 1:C], start=True, stop=True)
            last.then_inc(pieces_turned, 1)

            def gather(b):
                pe.wait_ge(path_ready, b + 1)
                pe.wait_ge(third_part, b + 1)
                for q in range(Q):
                    n = b * Q + q
                    if n == 0:
                        pe.wait_ge(squares_ready, B)
                    if n >= 4:
                        pe.wait_ge(x2_ready, n - 3)
                    for part_, first in ((HI, True), (MID, False), (LO, False)):
                        last = t.matmul(bank[4 + n % 4][:, :], path[b % 2][:, q * P:q * P + P], part_[:, b, :],
                                        start=first, stop=(part_ is LO))
                    last.then_inc(gathered, 1)

            def turn2(b):
                for q in range(Q):
                    pe.wait_ge(y2_ready, b * Q + q + 1)
                    for k in range(K):
                        if b == 0 and q == k == 0:
                            pe.wait_ge(weights_copied, 2 * NF)
                        if b >= 1 and q == 0:
                            pe.wait_ge(y2_copied, (b - 1) * K + k + 1)
                        ins = t.transpose(bank[k][:, q * P:q * P + P], ybuf[:, q, k * P:k * P + P], ident[:, :])
                        if q == Q - 1:
                            ins.then_inc(y2_turned, 1)

            def spread(n):
                pe.wait_ge(max_ready, n + 1)
                t.transpose(bank[7][0:1, 0:P], ymax[:, NT + n:NT + n + 1], ident[:, :]).then_inc(max_turned, 1)
                pe.wait_ge(step_ready, n + 1)
                t.matmul(bank[6][:, 0:2], onesr[:, :], qrow[:, 1:3], start=True, stop=True).then_inc(step_spread, 1)

            gather(0)
            gather(1)
            for b in range(B):
                if b + 2 < B:
                    gather(b + 2)
                elif b == B - 1:
                    pe.wait_ge(x2_ready, B * Q)
                    spread(0)
                turn2(b)
            pe.wait_ge(step_copied, 1)
            def first_layer(b, tokens):
                pe.wait_ge(tokens_rounded, b + 1)
                for f in range(NF):
                    if not isinstance(b, int) or b * NF + f >= 8:
                        pe.wait_ge(hidden_ready, b * NF + f - 7)
                    elif f >= 4:
                        pe.wait_ge(y2_copied, (B - 1) * K + f - 3)
                    for k in range(K):
                        last = t.matmul(bank[(f + 4) % 8][:, :], W1[:, k, f * P:f * P + P], tokens(k),
                                        start=(k == 0), stop=(k == K - 1))
                    last.then_inc(layer1_done, 1)

            first_layer(0, lambda k: XQ[:, 0, k, :])
            with pe.Fori(1, B) as b:
                first_layer(b, lambda k: XQF[:, bass.ds((b * K + k) * S, S)])
            def keep_awake(n):
                for _ in range(n):
                    t.matmul(bank[4][:, :], identb[:, :], W2[:, 0, :], start=True, stop=True)

            pe.wait_ge(hidden_ready, B * NF - 7)
            keep_awake(9)
            pe.wait_ge(hidden_ready, B * NF)
            spread(1)
            keep_awake(5)
            for g in range(4):
                for q in range(Q):
                    for f in range(4 * g, 4 * g + 4):
                        if q == 0:
                            pe.wait_ge(hidden_rounded, f + 1 if g == 0 else g + 4)
                        last = t.matmul(bank[q][:, :], HQ[:, 0, f, q * P:q * P + P], W2[:, f, :],
                                        start=(f == 0), stop=(f == NF - 1))
                    if g == 3:
                        last.then_inc(layer2_done, 1)

            def second_layer(i, odd):
                for q in range(Q):
                    if not isinstance(i, int):
                        pe.wait_ge(output_scaled, i * Q + q - 7)
                    for f in range(NF):
                        if q == 0 and f % 4 == 0:
                            pe.wait_ge(hidden_rounded, i * 4 + (f // 4 + 4))
                        last = t.matmul(bank[4 * odd + q][:, :], HQ[:, odd, f, q * P:q * P + P], W2[:, f, :],
                                        start=(f == 0), stop=(f == NF - 1))
                    last.then_inc(layer2_done, 1)

            second_layer(1, 1)
            with pe.Fori(2, B, 2) as i:
                second_layer(i, 0)
                second_layer(i + 1, 1)


_INS = ["x", "ctx_1024", "L0_ffn_w1", "L0_ffn_b1", "L0_ffn_w2", "L0_ffn_b2"]


def kernel(**inputs):
    import numpy as np
    import concourse.bacc as bacc
    from concourse.bass_utils import run_bass_kernel_spmd as run

    nc = bacc.Bacc("TRN2", target_bir_lowering=False, num_devices=1, dynamic_dma_scratch_size=1024)
    arrays, args = {}, []
    for name in _INS:
        arrays[f"in_{name}"] = np.ascontiguousarray(inputs[name])
    for name, a in constants(np).items():
        arrays[f"const_{name}"] = a
    for name, a in arrays.items():
        args.append(nc.dram_tensor(name, a.shape, mybir.dt.from_np(a.dtype), kind="ExternalInput").ap())
    out = nc.dram_tensor("out_0", (B, S, D), F32, kind="ExternalOutput").ap()
    build(nc, *args, out)
    r = run(nc, [arrays], core_ids=[0])
    return r.results[0]["out_0"]
```
